# Optimizing a Trainium2 kernel written in Bass

```python
import numpy as np
import jax
import jax.numpy as jnp

def _softmax(x, axis=-1):
    return jax.nn.softmax(x, axis=axis)

def _gelu(x):
    return jax.nn.gelu(x, approximate=True)

def _silu(x):
    return jax.nn.silu(x)

def _sigmoid(x):
    return jax.nn.sigmoid(x)

def _layernorm(x, axis=-1, eps=1e-05):
    m = jnp.mean(x, axis=axis, keepdims=True)
    v = jnp.var(x, axis=axis, keepdims=True)
    return (x - m) / jnp.sqrt(v + eps)

def _scatter_add(tgt, idx, src, axis=0):
    return tgt.at[idx].add(src)

def _segment_sum(src, seg, n):
    return jax.ops.segment_sum(src, seg, n)
kernel_name = 'mk_prb_d1_jaxref_r8_fa15f6'

def setup_inputs(seed: int=0):
    np.random.seed(seed)
    _w = jnp.asarray

    def _L0_attn_setup():
        import jax, jax.numpy as jnp
        import numpy as np
        NUM_HEADS = 16
        HEAD_DIM = 64
        NEG_INF = -1000000000.0

        def rotary_embedding(x, seq_len, head_dim):
            positions = jnp.arange(seq_len)
            dim_pairs = jnp.arange(0, head_dim, 2)
            freqs = 1.0 / 10000.0 ** (dim_pairs / head_dim)
            angles = positions[:, None] * freqs[None, :]
            cos = jnp.cos(angles)[:, None, :]
            sin = jnp.sin(angles)[:, None, :]
            x1 = x[..., ::2]
            x2 = x[..., 1::2]
            out1 = x1 * cos - x2 * sin
            out2 = x1 * sin + x2 * cos
            return jnp.stack([out1, out2], axis=-1).reshape(x.shape)
        key = jax.random.key(seed)
        k1, k2, k3 = jax.random.split(key, 3)
        batch, seq_len, embed_dim = (2, 256, 128)
        x = jax.random.normal(k1, (batch, seq_len, embed_dim), dtype=jnp.float32)
        W_qkv = jax.random.normal(k2, (embed_dim, 3 * NUM_HEADS * HEAD_DIM), dtype=jnp.float32) * 0.02
        W_out = jax.random.normal(k3, (NUM_HEADS * HEAD_DIM, embed_dim), dtype=jnp.float32) * 0.02
        return {'x': x, 'W_qkv': W_qkv, 'W_out': W_out}
    _L0_attn_in = _L0_attn_setup()

    def _L0_ffn_setup():
        import jax, jax.numpy as jnp
        import numpy as np
        H = 16
        EPS = 1e-05

        def layernorm(x, g, b):
            m = jnp.mean(x, axis=-1, keepdims=True)
            v = jnp.mean((x - m) ** 2, axis=-1, keepdims=True)
            return (x - m) * jax.lax.rsqrt(v + EPS) * g + b
        key = jax.random.key(seed)
        B, S, D, E = (4, 256, 128, 8)
        ks = jax.random.split(key, 16)
        s = 0.02
        inp = {'x': jax.random.normal(ks[0], (B, S, D), jnp.float32), 'Wq': jax.random.normal(ks[1], (D, D), jnp.float32) * s, 'bq': jnp.zeros((D,), jnp.float32), 'Wk': jax.random.normal(ks[2], (D, D), jnp.float32) * s, 'bk': jnp.zeros((D,), jnp.float32), 'Wv': jax.random.normal(ks[3], (D, D), jnp.float32) * s, 'bv': jnp.zeros((D,), jnp.float32), 'Wo': jax.random.normal(ks[4], (D, D), jnp.float32) * s, 'bo': jnp.zeros((D,), jnp.float32), 'g1': jnp.ones((D,), jnp.float32), 'be1': jnp.zeros((D,), jnp.float32), 'g2': jnp.ones((D,), jnp.float32), 'be2': jnp.zeros((D,), jnp.float32), 'Wg': jax.random.normal(ks[5], (D, E), jnp.float32) * s, 'bg': jnp.zeros((E,), jnp.float32), 'We': jax.random.normal(ks[6], (E, D, D), jnp.float32) * s, 'bexp': jnp.zeros((E, D), jnp.float32)}
        return inp
    _L0_ffn_in = _L0_ffn_setup()
    _d = {'L0_attn_x': _L0_attn_in['x'], 'L0_attn_W_qkv': _L0_attn_in['W_qkv'], 'L0_attn_W_out': _L0_attn_in['W_out'], 'L0_ffn_Wq': _L0_ffn_in['Wq'], 'L0_ffn_bq': _L0_ffn_in['bq'], 'L0_ffn_Wk': _L0_ffn_in['Wk'], 'L0_ffn_bk': _L0_ffn_in['bk'], 'L0_ffn_Wv': _L0_ffn_in['Wv'], 'L0_ffn_bv': _L0_ffn_in['bv'], 'L0_ffn_Wo': _L0_ffn_in['Wo'], 'L0_ffn_bo': _L0_ffn_in['bo'], 'L0_ffn_g1': _L0_ffn_in['g1'], 'L0_ffn_be1': _L0_ffn_in['be1'], 'L0_ffn_g2': _L0_ffn_in['g2'], 'L0_ffn_be2': _L0_ffn_in['be2'], 'L0_ffn_Wg': _L0_ffn_in['Wg'], 'L0_ffn_bg': _L0_ffn_in['bg'], 'L0_ffn_We': _L0_ffn_in['We'], 'L0_ffn_bexp': _L0_ffn_in['bexp']}
    _x0 = _d['L0_attn_x']
    _d['L0_attn_x'] = jax.random.normal(jax.random.fold_in(jax.random.key(seed), 1), (8, 512, 128), dtype=_x0.dtype)
    del _x0
    return _d

def reference(L0_attn_x, L0_attn_W_qkv, L0_attn_W_out, L0_ffn_Wq, L0_ffn_bq, L0_ffn_Wk, L0_ffn_bk, L0_ffn_Wv, L0_ffn_bv, L0_ffn_Wo, L0_ffn_bo, L0_ffn_g1, L0_ffn_be1, L0_ffn_g2, L0_ffn_be2, L0_ffn_Wg, L0_ffn_bg, L0_ffn_We, L0_ffn_bexp):

    def _L0_attn_ref(x, W_qkv, W_out):
        import jax, jax.numpy as jnp
        import numpy as np
        NUM_HEADS = 16
        HEAD_DIM = 64
        NEG_INF = -1000000000.0

        def rotary_embedding(x, seq_len, head_dim):
            positions = jnp.arange(seq_len)
            dim_pairs = jnp.arange(0, head_dim, 2)
            freqs = 1.0 / 10000.0 ** (dim_pairs / head_dim)
            angles = positions[:, None] * freqs[None, :]
            cos = jnp.cos(angles)[:, None, :]
            sin = jnp.sin(angles)[:, None, :]
            x1 = x[..., ::2]
            x2 = x[..., 1::2]
            out1 = x1 * cos - x2 * sin
            out2 = x1 * sin + x2 * cos
            return jnp.stack([out1, out2], axis=-1).reshape(x.shape)
        batch, seq_len, embed_dim = x.shape
        qkv = jnp.einsum('bse,ef->bsf', x, W_qkv)
        qkv = qkv.reshape(batch, seq_len, 3, NUM_HEADS, HEAD_DIM)
        q, k, v = (qkv[:, :, 0], qkv[:, :, 1], qkv[:, :, 2])
        q = rotary_embedding(q, seq_len, HEAD_DIM)
        k = rotary_embedding(k, seq_len, HEAD_DIM)
        scale = 1.0 / jnp.sqrt(jnp.asarray(HEAD_DIM, dtype=x.dtype))
        scores = jnp.einsum('bqhd,bkhd->bhqk', q, k) * scale
        mask = jnp.tril(jnp.ones((seq_len, seq_len), dtype=bool))[None, None, :, :]
        scores = jnp.where(mask, scores, NEG_INF)
        weights = jax.nn.softmax(scores, axis=-1)
        out = jnp.einsum('bhqk,bkhd->bqhd', weights, v)
        out = out.reshape(batch, seq_len, NUM_HEADS * HEAD_DIM)
        return jnp.einsum('bsf,fe->bse', out, W_out)

    def _L0_ffn_ref(x, Wq, bq, Wk, bk, Wv, bv, Wo, bo, g1, be1, g2, be2, Wg, bg, We, bexp):
        import jax, jax.numpy as jnp
        import numpy as np
        H = 16
        EPS = 1e-05

        def layernorm(x, g, b):
            m = jnp.mean(x, axis=-1, keepdims=True)
            v = jnp.mean((x - m) ** 2, axis=-1, keepdims=True)
            return (x - m) * jax.lax.rsqrt(v + EPS) * g + b
        B, S, D = x.shape
        Dh = D // H
        TOP_K = 2
        q = (x @ Wq + bq).reshape(B, S, H, Dh)
        k = (x @ Wk + bk).reshape(B, S, H, Dh)
        v = (x @ Wv + bv).reshape(B, S, H, Dh)
        scores = jnp.einsum('bqhd,bkhd->bhqk', q, k) / jnp.sqrt(jnp.float32(Dh))
        attn = jax.nn.softmax(scores, axis=-1)
        ctx = jnp.einsum('bhqk,bkhd->bqhd', attn, v).reshape(B, S, D)
        attn_out = ctx @ Wo + bo
        x = x + layernorm(attn_out, g1, be1)
        gate_probs = jax.nn.softmax(x @ Wg + bg, axis=-1)
        top_vals, top_idx = jax.lax.top_k(gate_probs, TOP_K)
        all_out = jnp.einsum('bsd,edf->bsef', x, We) + bexp
        picked = jnp.take_along_axis(all_out, top_idx[..., None], axis=2)
        moe_out = jnp.sum(top_vals[..., None] * picked, axis=2)
        return x + layernorm(moe_out, g2, be2)
    x = L0_attn_x
    xn = _layernorm(x, axis=-1)
    x = x + _L0_attn_ref(xn, L0_attn_W_qkv, L0_attn_W_out) + _L0_ffn_ref(xn, L0_ffn_Wq, L0_ffn_bq, L0_ffn_Wk, L0_ffn_bk, L0_ffn_Wv, L0_ffn_bv, L0_ffn_Wo, L0_ffn_bo, L0_ffn_g1, L0_ffn_be1, L0_ffn_g2, L0_ffn_be2, L0_ffn_Wg, L0_ffn_bg, L0_ffn_We, L0_ffn_bexp)
    return x

_drawn_inputs = setup_inputs


def setup_inputs(seed=0):
    import zlib

    import numpy as np

    out = dict(_drawn_inputs(seed))
    spreads = {'L0_ffn_bq': (0.0, 2.0),
     'L0_ffn_bk': (0.0, 2.0),
     'L0_ffn_bv': (0.0, 0.1),
     'L0_ffn_bo': (0.0, 0.1),
     'L0_ffn_g1': (1.0, 0.2),
     'L0_ffn_be1': (0.0, 0.1),
     'L0_ffn_g2': (1.0, 0.2),
     'L0_ffn_be2': (0.0, 0.428),
     'L0_ffn_bg': (0.0, 0.1),
     'L0_ffn_bexp': (0.0, 0.1)}
    factors = {'L0_attn_W_qkv': 8.0, 'L0_attn_W_out': 8.0, 'L0_ffn_Wq': 3.814, 'L0_ffn_Wk': 3.443}
    for name, (base, spread) in spreads.items():
        noise = np.random.default_rng([zlib.crc32(name.encode()), seed]).standard_normal(out[name].shape)
        drawn = base * np.exp(spread * noise) if base else spread * noise
        out[name] = jnp.asarray(drawn.astype(out[name].dtype))
    for name, factor in factors.items():
        out[name] = (out[name] * factor).astype(out[name].dtype)
    return out
```

```python
import concourse.bass as bass
from concourse import mybir
from contextlib import ExitStack
import math

F32 = mybir.dt.float32
F32R = mybir.dt.float32r
BF16 = mybir.dt.bfloat16
U32 = mybir.dt.uint32
ALU = mybir.AluOpType
ACT = mybir.ActivationFunctionType
AX = mybir.AxisListType

B, S, D = 8, 512, 128
P = 128
T = S // P
H, DH = 16, 64
FH, FD = 16, 8
PH = 2
PG = H // PH
GH = 4
G = FH // GH
E = 8
STRIP = 32
EPS = 1e-5
VW, FVW = DH + 1, FD + 1
BLOCKS = H * DH // P
HALF = 512 // D

BIAS = {"bexp": (0, 0, E * D), "bq": (32, 0, FH * STRIP), "bk": (64, 0, FH * STRIP),
        "bv": (96, 0, D), "bo": (96, D, D), "bg": (96, 2 * D, E)}
ONES = E * D
BIAS_N = ONES + P

C_ID, C_MS, C_MT, C_COL, C_IOTA = 0, P, 2 * P, 3 * P, 3 * P + 4
C_N = C_IOTA + E

SM_UNITS = [[(3, 0)], [(2, 0), (0, 3 * P)], [(1, 0)]]
ST_UNITS = [[(0, 0)], [(1, 0), (3, 3 * P)], [(2, 0)]]
ST_N = [S, S, 2 * P]
PT_AT = [0, S, 2 * S, S + 3 * P]


def batch_plan():
    plan = [("xT",), ("proj", 0, 0), ("proj", 0, 1), ("fq", 0), ("fk", 0), ("fv",)]
    plan += [("v", t, half) for t in range(T) for half in range(2)]
    for s in range(H + 7):
        wk, sm, st, pv = [], [], [], []
        if 0 <= s - 2 < H:
            wk.append(("mT", s - 2))
        if s >= 5 and (s - 5) % GH == 0 and (s - 5) // GH < G:
            wk.insert(0, ("fmT", (s - 5) // GH))
        if s < H:
            wk += [("tq", s), ("tk", s)]
        if s // PH + 1 < PG:
            wk.append(("proj", s // PH + 1, s % PH))
        if s < H and s % GH == 2 and s // GH + 1 < G:
            wk += [("fq", s // GH + 1), ("fk", s // GH + 1)]
        if s >= 6 and s % 2 == 0 and (s - 6) // 2 < BLOCKS:
            wk.append(("oT", (s - 6) // 2))
        if s >= 7 and (s - 7) % 2 == 0 and (s - 7) // 2 < BLOCKS:
            wk.append(("attn", (s - 7) // 2))
        if 0 <= s - 1 < H:
            sm = [("sm", s - 1, u) for u in range(3)] + [("fsm", s - 1, j) for j in range(T)]
        if 0 <= s - 3 < H:
            st += [("st", s - 3, u) for u in range(3)]
        if 0 <= s - 6 < FH:
            st += [("fst", s - 6, i) for i in range(T)]
        if 0 <= s - 4 < H:
            pv += [("pv", s - 4, j) for j in range(T)]
        if 0 <= s - 7 < FH:
            pv += [("fpv", s - 7, j) for j in range(T)]
        lists = [st, wk, sm, pv]
        most = max(map(len, lists))
        for k in range(most):
            for x in lists:
                lo, hi = k * len(x) // most, (k + 1) * len(x) // most
                plan += x[lo:hi]
    plan += [("cT",), ("wo",), ("x2T",), ("gate",)]
    plan += [("moe", t, half) for t in range(T) for half in range(2)]
    return plan


PLAN = batch_plan()
WK_KINDS = ("xT", "v", "fv", "fq", "fk", "proj", "tq", "tk", "mT", "fmT", "oT", "attn", "cT", "wo", "x2T", "gate", "moe")
SPLIT_KINDS = ("xT", "fq", "fk", "tq", "tk", "oT", "cT", "x2T")


def numbered(choose):
    return {x: n + 1 for n, x in enumerate(x for x in PLAN if choose(x))}


WK = numbered(lambda x: x[0] in WK_KINDS)
SM = numbered(lambda x: x[0] in ("sm", "fsm"))
ST = numbered(lambda x: x[0] in ("st", "fst"))
SPLIT = numbered(lambda x: x[0] in SPLIT_KINDS)
PROJ = numbered(lambda x: x[0] == "proj")
V_ACT = numbered(lambda x: x[0] == "v" and x[2] == 0)
V_DVE = numbered(lambda x: x[0] == "fv" or (x[0] == "v" and x[2] == 1))
WK_LIST = list(WK)
assert len(WK) % 2 == 0
MISC = numbered(lambda x: x[0] in ("attn", "wo", "gate", "moe"))
N_STEP = 49


def build(nc, x, w_qkv, w_out, wq, bq, wk, bk, wv, bv, wo, bo, g1, be1, g2, be2, wg, bg, we, bexp, table, rope, out):
    with ExitStack() as ctx:
        def sb(name, shape, dt=F32):
            return ctx.enter_context(nc.sbuf_tensor(name, shape, dt))

        def sem(name):
            return ctx.enter_context(nc.semaphore(name))

        consts = sb("consts", [P, C_N])
        ident = consts[:, C_ID:C_ID + P]
        low_rows = consts[:, C_COL:C_COL + 1]
        q_low = consts[:, C_COL + 1:C_COL + 2]
        k_low = consts[:, C_COL + 2:C_COL + 3]
        second = consts[:, C_COL + 3:C_COL + 4]
        experts = consts[:, C_IOTA:C_IOTA + E]
        masks = sb("masks", [P, 3, P], BF16)
        angles = sb("angles", [P, T, 3 * DH // 2])
        wqkv_h = sb("wqkv_h", [P, 3 * H * DH], F32R)
        wqkv_l = sb("wqkv_l", [P, 3 * H * DH], F32R)
        wout_h = sb("wout_h", [P, BLOCKS, D], F32R)
        wout_l = sb("wout_l", [P, BLOCKS, D], F32R)
        we_h = sb("we_h", [P, E, D], F32R)
        we_l = sb("we_l", [P, E, D], F32R)
        small_h = sb("small_h", [P, 2 * D + E], F32R)
        small_l = sb("small_l", [P, 2 * D + E], F32R)
        strips_h = sb("strips_h", [P, 2, FH, STRIP], F32R)
        strips_l = sb("strips_l", [P, 2, FH, STRIP], F32R)
        affine = sb("affine", [P, 4, D])
        biases = sb("biases", [P, BIAS_N], F32R)

        x_in = sb("x_in", [P, T, D])
        xn = sb("xn", [P, T, D])
        xt_h = sb("xt_h", [P, S], F32R)
        xt_l = sb("xt_l", [P, S], F32R)
        v = sb("v", [P, T, H, VW])
        fv = sb("fv", [P, T, FH, FVW])
        rot = sb("rot", [P, 2, 2, 2 * PH * DH])
        qk = sb("qk", [P, 2, T, 2 * PH, 2, DH])
        q_hl = sb("q_hl", [P, 4, S], F32R)
        q_hm = sb("q_hm", [P, 4, S], F32R)
        k_hh = sb("k_hh", [P, 4, S], F32R)
        k_l1 = sb("k_l1", [P, 4, S], F32R)
        fq = sb("fq", [P, 3, S], F32R)
        fk = sb("fk", [P, 3, S], F32R)
        nmax = sb("nmax", [P, 4, T])
        fnmax = sb("fnmax", [P, T, GH, STRIP])
        pt = sb("pt", [P, 2, 2 * S + 2 * P])
        fpt = sb("fpt", [P, 2, T, S])
        rec = sb("rec", [P, T])
        frec = sb("frec", [P, GH, T])
        o = sb("o", [P, T, 4, D])
        ot_h = sb("ot_h", [P, 2, S], F32R)
        ot_l = sb("ot_l", [P, 2, S], F32R)
        ct = sb("ct", [P, T, D])
        ct_h = sb("ct_h", [P, S], F32R)
        ct_l = sb("ct_l", [P, S], F32R)
        x2 = xn
        x2t_h, x2t_l = ct_h, ct_l
        y = sb("y", [P, T, D])
        branch = ct
        weighted = rot[:].rearrange("p a c (e d) -> p (a c e) d", d=D)
        result = sb("result", [P, T, D])
        stats = sb("stats", [P, T, 6])
        moments = sb("moments", [P, T, 2])
        spread = sb("spread", [P, T])
        rstd = sb("rstd", [P, T])
        power = sb("power", [P, T])
        spare = sb("spare", [P, 1])
        gmax = sb("gmax", [P, T])
        gsum = sb("gsum", [P, T])
        grec = sb("grec", [P, T])
        glog = sb("glog", [P, T, E])
        gexp = sb("gexp", [P, T, E])
        gprob = sb("gprob", [P, T, E])
        gtop = sb("gtop", [P, T, E])
        gidx = sb("gidx", [P, T, E], U32)
        gidf = sb("gidf", [P, T, E])
        gate_a = sb("gate_a", [P, T, E])
        gate_b = sb("gate_b", [P, T, E])
        gate_w = sb("gate_w", [P, T, E])
        qk_flat = qk[:].rearrange("p a t h r d -> p (a t h r d)")
        rot_flat = rot[:].rearrange("p a c n -> p (a c n)")
        raw_qkv = fpt[:].rearrange("p a t n -> p (a t n)")[:, 0:3 * H * DH]
        raw_out = qk_flat[:, 0:BLOCKS * D].rearrange("p (c n) -> p c n", n=D)
        raw_we = qk_flat[:, BLOCKS * D:BLOCKS * D + E * D].rearrange("p (e n) -> p e n", n=D)
        raw_small = rot_flat[:, 0:2 * D + E]
        raw_qk = rot_flat[:, 512:512 + 2 * D]
        raw_bias = pt[:].rearrange("p a n -> p (a n)")[:, 0:BIAS_N]
        hi_bias = v[:].rearrange("p t h d -> p (t h d)")[:, 0:BIAS_N].bitcast(F32R)

        wk_bank = [ctx.enter_context(nc.psum_tensor(f"wk{i}", [P, 512], F32)) for i in range(2)]
        sm_bank = [ctx.enter_context(nc.psum_tensor(f"sm{i}", [P, 512], F32)) for i in range(2)]
        st_bank = [ctx.enter_context(nc.psum_tensor(f"st{i}", [P, 512], F32)) for i in range(2)]
        pv_bank = ctx.enter_context(nc.psum_tensor("pv_bank", [P, 512], F32))
        fpv_bank = ctx.enter_context(nc.psum_tensor("fpv_bank", [P, 512], F32))

        loaded = sem("loaded")
        x_loaded = sem("x_loaded")
        out_sent = sem("out_sent")
        prepared = sem("prepared")
        prep_pool = sem("prep_pool")
        prep_dve = sem("prep_dve")
        events = {}

        def per_batch(name, n):
            s = sem(name)
            events[id(s)] = n
            return s

        wk_full = per_batch("wk_full", len(WK))
        sm_full = per_batch("sm_full", len(SM))
        st_full = per_batch("st_full", len(ST))
        pv_full = per_batch("pv_full", H)
        fpv_full = per_batch("fpv_full", FH)
        rounded = per_batch("rounded", len(SPLIT))
        v_act = per_batch("v_act", len(V_ACT))
        max_row_done = per_batch("max_row_done", H)
        exp_done = per_batch("exp_done", len(ST))
        gate_exp = per_batch("gate_exp", 1)
        split = per_batch("split", len(SPLIT))
        v_dve = per_batch("v_dve", len(V_DVE))
        turned = per_batch("turned", 2 * len(PROJ))
        rotated = per_batch("rotated", 2 * len(PROJ))
        variance = per_batch("variance", 3)
        rstd_done = per_batch("rstd_done", 3)
        max_done = per_batch("max_done", len(SM))
        fmax_done = per_batch("fmax_done", G)
        normed = per_batch("normed", H)
        fnormed = per_batch("fnormed", G)
        misc_read = per_batch("misc_read", len(MISC))
        normal = per_batch("normal", 1)
        x2_done = per_batch("x2_done", 1)
        logits = per_batch("logits", 1)
        result_done = per_batch("result_done", 1)
        step_done = per_batch("step_done", N_STEP)

        def now(b, s, c):
            n = events[id(s)]
            assert 1 <= c <= n, (c, n)
            return b * n + (n + c)

        def past(b, s, c):
            n = events[id(s)]
            assert 1 <= c <= n, (c, n)
            return b * n + c

        def since(b, s, c):
            return now(b, s, c) if c >= 1 else past(b, s, c + events[id(s)])

        def start(eng, *sems):
            for s in sems:
                eng.sem_inc(s, events[id(s)])

        def wk_of(x):
            return wk_bank[(WK[x] - 1) % 2]

        def wk_freed(x):
            if x in SPLIT:
                return split, SPLIT[x]
            if x in V_ACT:
                return v_act, V_ACT[x]
            if x in V_DVE:
                return v_dve, V_DVE[x]
            if x in PROJ:
                return turned, 2 * PROJ[x]
            if x[0] == "mT":
                return max_row_done, x[1] + 1
            if x[0] == "fmT":
                return fmax_done, x[1] + 1
            return misc_read, MISC[x]

        x_tiles = x.rearrange("b (t p) d -> b p t d", p=P)
        out_tiles = out.rearrange("b (t p) d -> b p t d", p=P)
        N_LOADS = 14 + 2 * (4 + 6)

        block = ctx.enter_context(nc.Block())

        @block.sync
        def _(sp):
            sp.dma_start(x_in[:], x_tiles[0]).then_inc(x_loaded, 16)
            loads = [
                (raw_qkv, w_qkv), (consts[:], table), (angles[:], rope.rearrange("(t p) c -> p t c", p=P)),
                (raw_small[:, 0:D], wv), (raw_small[:, D:2 * D], wo), (raw_small[:, 2 * D:2 * D + E], wg),
                (raw_qk[:, 0:D], wq), (raw_qk[:, D:2 * D], wk),
                (raw_we, we.rearrange("e d f -> d e f")), (raw_out, w_out.rearrange("(c p) n -> p c n", p=P)),
            ]
            for n, a in enumerate((g1, be1, g2, be2)):
                loads.append((affine[:, n, :], a.rearrange("(a d) -> a d", a=1).broadcast_to([P, D])))
            for r in range(2):
                for name, a in (("bv", bv), ("bo", bo), ("bg", bg), ("bexp", bexp.rearrange("e d -> (e d)"))):
                    p0, at, n = BIAS[name]
                    loads.append((raw_bias[p0 + r:p0 + r + 1, at:at + n], a.rearrange("(a d) -> a d", a=1)))
                for name, a in (("bq", bq), ("bk", bk)):
                    p0, at, n = BIAS[name]
                    strip = raw_bias[p0 + r:p0 + r + 1, at:at + n].rearrange("p (h c) -> p h c", c=STRIP)
                    for c in range(1, 4):
                        loads.append((strip[:, :, c * FD:(c + 1) * FD], a.rearrange("(a h d) -> a h d", a=1, d=FD)))
            sp.wait_ge(prepared, 1)
            for dst, src in loads:
                sp.dma_start(dst, src).then_inc(loaded, 16)
            assert len(loads) == N_LOADS
            with sp.Fori(0, B - 1) as b:
                sp.wait_ge(normal, now(b, normal, 1))
                sp.dma_start(x_in[:], x_tiles[bass.ds(b + 1, 1)].rearrange("b p t d -> p (b t) d")).then_inc(x_loaded, 16)
                sp.wait_ge(result_done, now(b, result_done, 1))
                sp.dma_start(out_tiles[bass.ds(b, 1)].rearrange("b p t d -> p (b t) d"), result[:]).then_inc(out_sent, 16)
            sp.wait_ge(result_done, now(B - 1, result_done, 1))
            sp.dma_start(out_tiles[B - 1], result[:]).then_inc(out_sent, 16)
            sp.wait_ge(out_sent, 16 * (B + 1))

        @block.gpsimd
        def _(pool):
            nc.gpsimd.memset(power[:], -0.5).then_inc(prep_pool, 1)
            pool.wait_ge(prep_pool, 1)
            start(pool, rotated, rstd_done)

            def root(b, n):
                pool.wait_ge(variance, now(b, variance, n))
                nc.gpsimd.tensor_tensor(rstd[:], spread[:], power[:], ALU.pow).then_inc(rstd_done, 1)

            with pool.Fori(0, B) as b:
                root(b, 1)
                for x_ in PLAN:
                    if x_[0] == "proj":
                        _, g, pair = x_
                        for k in range(2):
                            t, n = 2 * pair + k, 2 * PROJ[x_] - 1 + k
                            pool.wait_ge(turned, now(b, turned, n))
                            if t == 0:
                                last = WK[("tk", PH * ((g - 2) % PG) + PH - 1)]
                                pool.wait_ge(wk_full, since(b, wk_full, last if g >= 2 else last - len(WK)))
                            shape = [P, 2 * PH, 2, DH // 2]
                            c, s_ = (rot[:, n % 2, m].rearrange("p (h i two) -> p h i two", two=2, i=DH // 2) for m in range(2))
                            dst = qk[:, g % 2, t].rearrange("p h r (two i) -> p h r two i", two=2)
                            for two in range(2):
                                ins = nc.gpsimd.tensor_tensor(
                                    dst[:, :, :, two], c[:, :, :, two].unsqueeze(2).broadcast_to(shape),
                                    s_[:, :, :, 1 - two].unsqueeze(2).broadcast_to(shape), ALU.add)
                            ins.then_inc(rotated, 1)
                    elif x_[0] == "wo":
                        root(b, 2)
                root(b, 3)

        @block.scalar
        def _(act):
            act.wait_ge(loaded, 16 * N_LOADS)
            nc.scalar.copy(wqkv_h[:], raw_qkv).then_inc(prepared, 1)
            nc.scalar.copy(wout_h[:], raw_out).then_inc(prepared, 1)
            nc.scalar.copy(we_h[:], raw_we).then_inc(prepared, 1)
            nc.scalar.copy(small_h[:], raw_small).then_inc(prepared, 1)
            start(act, rounded, v_act, max_row_done, exp_done, gate_exp)
            f_scale = 1.0 / math.sqrt(FD)
            with act.Fori(0, B) as b:
                for x_ in PLAN:
                    kind = x_[0]
                    if kind in SPLIT_KINDS:
                        act.wait_ge(wk_full, now(b, wk_full, WK[x_]))
                        src = wk_of(x_)[:]
                        if kind == "xT":
                            act.wait_ge(wk_full, past(b, wk_full, max(WK[("fk", G - 1)], WK[("proj", PG - 1, 1)], WK[("v", T - 1, 1)])))
                            dst = xt_h[:]
                        elif kind in ("fq", "fk"):
                            g = x_[1]
                            act.wait_ge(st_full, since(b, st_full, ST[("fst", GH * (g - 3) + GH - 1, T - 1)] if g >= 3 else
                                 ST[("fst", GH * (3 if g == 0 else g) + GH - 1, T - 1)] - len(ST)))
                            dst = (fq if kind == "fq" else fk)[:, g % 3]
                        elif kind in ("tq", "tk"):
                            h = x_[1]
                            last = ST[("st", (h - 4) % H, 2)]
                            act.wait_ge(st_full, since(b, st_full, last if h >= 4 else last - len(ST)))
                            dst = (q_hm if kind == "tq" else k_hh)[:, h % 4]
                        elif kind == "oT":
                            c = x_[1]
                            last = WK[("attn", (c - 2) % BLOCKS)]
                            act.wait_ge(wk_full, since(b, wk_full, last if c >= 2 else last - len(WK)))
                            dst = ot_h[:, c % 2]
                        elif kind == "cT":
                            act.wait_ge(wk_full, past(b, wk_full, WK[("wo",)]))
                            dst = ct_h[:]
                        else:
                            act.wait_ge(wk_full, past(b, wk_full, WK[("moe", T - 1, 1)]))
                            dst = x2t_h[:]
                        nc.scalar.copy(dst, src).then_inc(rounded, 1)
                    elif x_ in V_ACT:
                        _, t, half = x_
                        act.wait_ge(wk_full, now(b, wk_full, WK[x_]))
                        if t == 0:
                            act.wait_ge(pv_full, past(b, pv_full, H))
                        nc.scalar.copy(v[:, t, 0:H // 2, 0:DH],
                                           wk_of(x_)[:].rearrange("p (h d) -> p h d", d=DH)).then_inc(v_act, 1)
                    elif kind == "mT":
                        act.wait_ge(wk_full, now(b, wk_full, WK[x_]))
                        nc.scalar.copy(q_hm[64:65, x_[1] % 4], wk_of(x_)[64:65, :]).then_inc(max_row_done, 1)
                    elif kind == "st":
                        _, h, u = x_
                        act.wait_ge(st_full, now(b, st_full, ST[x_]))
                        if u == 0:
                            act.wait_ge(pv_full, since(b, pv_full, h - 1))
                        bank = st_bank[(ST[x_] - 1) % 2]
                        nc.scalar.activation(pt[:, h % 2, PT_AT[u]:PT_AT[u] + ST_N[u]], bank[:, 0:ST_N[u]],
                                                 ACT.Exp, scale=1.0 / math.sqrt(DH)).then_inc(exp_done, 1)
                    elif kind == "fst":
                        _, f, i = x_
                        act.wait_ge(st_full, now(b, st_full, ST[x_]))
                        if i == 0:
                            act.wait_ge(fpv_full, since(b, fpv_full, f - 1))
                        bank = st_bank[(ST[x_] - 1) % 2]
                        nc.scalar.activation(fpt[:, f % 2, i], bank[:], ACT.Exp, scale=f_scale).then_inc(exp_done, 1)
                    elif kind == "gate":
                        act.wait_ge(logits, now(b, logits, 1))
                        nc.scalar.activation(gexp[:], glog[:], ACT.Exp).then_inc(gate_exp, 1)

        @block.vector
        def _(dve):
            taken = [0]

            def next_step():
                taken[0] += 1
                return taken[0]

            nc.vector.memset(raw_bias, 0.0).then_inc(prepared, 1)
            nc.vector.memset(fnmax[:], 0.0)
            nc.vector.memset(k_l1[:].bitcast(F32), 1.0)
            nc.vector.memset(v[:].rearrange("p t h d -> p (t h) d")[:, :, DH:VW], 1.0)
            nc.vector.memset(fv[:].rearrange("p t h d -> p (t h) d")[:, :, FD:FVW], 1.0)
            nc.vector.memset(strips_h[:].bitcast(F32), 0.0)
            nc.vector.memset(strips_l[:].bitcast(F32), 0.0).then_inc(prep_dve, 1)
            dve.wait_ge(loaded, 16 * N_LOADS)
            row_k, at_k, n_k = BIAS["bk"]
            nc.vector.memset(raw_bias[row_k:row_k + 1, at_k:at_k + n_k].rearrange("p (h c) -> p h c", c=STRIP)[:, :, 0:1],
                             1.0).then_inc(prep_dve, 1)
            nc.vector.tensor_copy(masks[:], consts[:, 0:3 * P].rearrange("p (c n) -> p c n", n=P))
            dve.wait_ge(prep_dve, 2)
            nc.vector.tensor_copy(hi_bias, raw_bias).then_inc(prep_dve, 1)
            dve.wait_ge(prep_dve, 3)
            nc.vector.scalar_tensor_tensor(out=biases[:], in0=hi_bias.bitcast(F32), scalar=second, in1=raw_bias,
                                           op0=ALU.mult, op1=ALU.add).then_inc(prep_dve, 1)
            dve.wait_ge(prep_dve, 4)
            nc.vector.memset(biases[:, ONES:BIAS_N].bitcast(F32), 1.0)
            nc.vector.memset(biases[BIAS["bq"][0]:BIAS["bq"][0] + 2, S:2 * S].bitcast(F32), 1.0)
            nc.vector.memset(biases[BIAS["bk"][0]:BIAS["bk"][0] + 2, S:2 * S].bitcast(F32), 1.0)
            for n in range(2):
                src = raw_qk[:, n * D:(n + 1) * D].rearrange("p (h d) -> p h d", d=FD)
                for c in range(1, 4):
                    nc.vector.tensor_copy(strips_h[:, n, :, c * FD:(c + 1) * FD], src).then_inc(prep_dve, 1)
            dve.wait_ge(prep_dve, 10)
            for n in range(2):
                src = raw_qk[:, n * D:(n + 1) * D].rearrange("p (h d) -> p h d", d=FD)
                for c in range(1, 4):
                    nc.vector.tensor_tensor(strips_l[:, n, :, c * FD:(c + 1) * FD], src,
                                            strips_h[:, n, :, c * FD:(c + 1) * FD].bitcast(F32), ALU.subtract)
            dve.wait_ge(prepared, 5)
            nc.vector.tensor_tensor(wqkv_l[:], raw_qkv, wqkv_h[:].bitcast(F32), ALU.subtract)
            nc.vector.tensor_tensor(wout_l[:], raw_out, wout_h[:].bitcast(F32), ALU.subtract)
            nc.vector.tensor_tensor(we_l[:], raw_we, we_h[:].bitcast(F32), ALU.subtract)
            nc.vector.tensor_tensor(small_l[:], raw_small, small_h[:].bitcast(F32), ALU.subtract).then_inc(prep_dve, 1)
            nc.vector.memset(v[:].rearrange("p t h d -> p (t h) d")[:, :, DH:VW], 1.0).then_inc(prep_dve, 1)
            dve.wait_ge(prep_dve, 12)
            dve.drain().then_inc(prepared, 1)
            start(dve, variance, split, v_dve, turned, max_done, fmax_done, normed, fnormed, misc_read, normal, x2_done,
                  logits, result_done, step_done)

            def carry_wait():
                nc.vector.memset(spare[:], 0.0)

            norms = [0]

            def layernorm(b, src):
                for t in range(T):
                    ins = nc.vector.bn_stats(stats[:, t], src(t))
                ins.then_inc(step_done, 1)
                dve.wait_ge(step_done, now(b, step_done, next_step()))
                carry_wait()
                for t in range(T):
                    ins = nc.vector.bn_aggr(moments[:, t], stats[:, t])
                ins.then_inc(step_done, 1)
                dve.wait_ge(step_done, now(b, step_done, next_step()))
                nc.vector.tensor_scalar(spread[:].unsqueeze(2), moments[:, :, 1:2], EPS, None, ALU.add).then_inc(variance, 1)
                norms[0] += 1
                dve.wait_ge(rstd_done, now(b, rstd_done, norms[0]))

            with dve.Fori(0, B) as b:
                taken[0] = norms[0] = 0
                dve.wait_ge(x_loaded, b * 16 + 16)
                layernorm(b, lambda t: x_in[:, t])
                dve.wait_ge(wk_full, past(b, wk_full, WK[("x2T",)]))
                for t in range(T):
                    nc.vector.tensor_scalar(xn[:, t], x_in[:, t], moments[:, t, 0:1], rstd[:, t:t + 1],
                                            ALU.subtract, ALU.mult)
                nc.vector.tensor_copy(y[:], x_in[:]).then_inc(normal, 1)
                for x_ in PLAN:
                    kind = x_[0]
                    if kind in SPLIT_KINDS:
                        dve.wait_ge(rounded, now(b, rounded, SPLIT[x_]))
                        src = wk_of(x_)[:]
                        if kind == "xT":
                            ins = nc.vector.tensor_tensor(xt_l[:], src, xt_h[:].bitcast(F32), ALU.subtract)
                        elif kind in ("fq", "fk"):
                            strips = (fq if kind == "fq" else fk)[:, x_[1] % 3]
                            ins = nc.vector.scalar_tensor_tensor(
                                out=strips, in0=strips.bitcast(F32), scalar=q_low if kind == "fq" else k_low, in1=src,
                                op0=ALU.mult, op1=ALU.add)
                        elif kind == "tq":
                            h = x_[1]
                            ins = nc.vector.scalar_tensor_tensor(out=q_hl[:, h % 4], in0=q_hm[:, h % 4].bitcast(F32),
                                                                 scalar=low_rows, in1=src, op0=ALU.mult, op1=ALU.add)
                        elif kind == "tk":
                            h = x_[1]
                            ins = nc.vector.tensor_tensor(k_l1[0:DH, h % 4], src[0:DH], k_hh[0:DH, h % 4].bitcast(F32),
                                                          ALU.subtract)
                        elif kind == "oT":
                            c = x_[1]
                            ins = nc.vector.tensor_tensor(ot_l[:, c % 2], src, ot_h[:, c % 2].bitcast(F32), ALU.subtract)
                        elif kind == "cT":
                            ins = nc.vector.tensor_tensor(ct_l[:], src, ct_h[:].bitcast(F32), ALU.subtract)
                        else:
                            ins = nc.vector.tensor_tensor(x2t_l[:], src, x2t_h[:].bitcast(F32), ALU.subtract)
                        ins.then_inc(split, 1)
                    elif kind == "v" and x_ in V_DVE:
                        _, t, half = x_
                        dve.wait_ge(wk_full, now(b, wk_full, WK[x_]))
                        if t == 0:
                            dve.wait_ge(pv_full, past(b, pv_full, H))
                        nc.vector.tensor_copy(v[:, t, H // 2:H, 0:DH],
                                                  wk_of(x_)[:].rearrange("p (h d) -> p h d", d=DH)).then_inc(v_dve, 1)
                    elif kind == "fv":
                        dve.wait_ge(wk_full, now(b, wk_full, WK[x_]))
                        dve.wait_ge(fpv_full, past(b, fpv_full, FH))
                        nc.vector.tensor_copy(fv[:, :, :, 0:FD],
                                                  wk_of(x_)[:].rearrange("p (t h d) -> p t h d", t=T, d=FD)).then_inc(v_dve, 1)
                    elif kind == "proj":
                        _, g, pair = x_
                        dve.wait_ge(wk_full, now(b, wk_full, WK[x_]))
                        for k in range(2):
                            t, n = 2 * pair + k, 2 * PROJ[x_] - 1 + k
                            dve.wait_ge(rotated, since(b, rotated, n - 2))
                            w = 2 * PH * DH
                            src = wk_of(x_)[:, k * w:(k + 1) * w]
                            cos = angles[:, t, 0:DH // 2].unsqueeze(1).unsqueeze(3).broadcast_to([P, 2 * PH, DH // 2, 2])
                            sin = angles[:, t, DH // 2:].unsqueeze(1).broadcast_to([P, 2 * PH, DH])
                            nc.vector.tensor_tensor(rot[:, n % 2, 0].rearrange("p (h i two) -> p h i two", two=2, i=DH // 2),
                                                    src.rearrange("p (h i two) -> p h i two", two=2, i=DH // 2), cos, ALU.mult)
                            nc.vector.tensor_tensor(rot[:, n % 2, 1].rearrange("p (h d) -> p h d", d=DH),
                                                        src.rearrange("p (h d) -> p h d", d=DH), sin, ALU.mult).then_inc(turned, 1)
                    elif kind == "sm":
                        _, h, u = x_
                        dve.wait_ge(sm_full, now(b, sm_full, SM[x_]))
                        if u == 0:
                            last = WK[("mT", (h - 4) % H)]
                            dve.wait_ge(wk_full, since(b, wk_full, last if h >= 4 else last - len(WK)))
                        bank = sm_bank[(SM[x_] - 1) % 2]
                        for j, at in SM_UNITS[u]:
                            ins = nc.vector.tensor_reduce(nmax[:, h % 4, j:j + 1], bank[:, at:at + (j + 1) * P],
                                                          AX.X, ALU.max, negate=True)
                        ins.then_inc(max_done, 1)
                    elif kind == "fsm":
                        _, f, j = x_
                        dve.wait_ge(sm_full, now(b, sm_full, SM[x_]))
                        if f % GH == 0 and j == 0:
                            g = f // GH
                            last = WK[("fmT", (g - 1) % G)]
                            dve.wait_ge(wk_full, since(b, wk_full, last if g >= 1 else last - len(WK)))
                        bank = sm_bank[(SM[x_] - 1) % 2]
                        nc.vector.tensor_reduce(fnmax[:, j, f % GH, 0:1], bank[:],
                                                    AX.X, ALU.max, negate=True).then_inc(max_done, 1)
                    elif kind == "fmT":
                        g = x_[1]
                        dve.wait_ge(wk_full, now(b, wk_full, WK[x_]))
                        nc.vector.tensor_tensor(fq[:, g % 3], wk_of(x_)[:], fq[:, g % 3].bitcast(F32), ALU.add).then_inc(fmax_done, 1)
                    elif kind == "pv" and x_[2] == T - 1:
                        h = x_[1]
                        dve.wait_ge(pv_full, now(b, pv_full, h + 1))
                        sums = pv_bank[:, 0:T * VW].rearrange("p (j d) -> p j d", d=VW)
                        nc.vector.reciprocal(rec[:].unsqueeze(2), sums[:, :, DH:VW]).then_inc(step_done, 1)
                        dve.wait_ge(step_done, now(b, step_done, next_step()))
                        c = h // 2
                        if h % 2 == 0:
                            last = WK[("oT", (c - 4) % BLOCKS)]
                            dve.wait_ge(wk_full, since(b, wk_full, last if c >= 4 else last - len(WK)))
                        nc.vector.tensor_tensor(o[:, :, c % 4, h % 2 * DH:(h % 2 + 1) * DH], sums[:, :, 0:DH],
                                                    rec[:].unsqueeze(2).broadcast_to([P, T, DH]), ALU.mult).then_inc(normed, 1)
                    elif kind == "fpv" and x_[2] == T - 1 and x_[1] % GH == GH - 1:
                        g = x_[1] // GH
                        dve.wait_ge(fpv_full, now(b, fpv_full, x_[1] + 1))
                        sums = fpv_bank[:, 0:GH * T * FVW].rearrange("p (f j d) -> p f j d", f=GH, d=FVW)
                        nc.vector.reciprocal(frec[:].unsqueeze(3), sums[:, :, :, FD:FVW]).then_inc(step_done, 1)
                        dve.wait_ge(step_done, now(b, step_done, next_step()))
                        if g == 0:
                            dve.wait_ge(wk_full, past(b, wk_full, WK[("cT",)]))
                        dst = ct[:, :, g * GH * FD:(g + 1) * GH * FD].rearrange("p j (f d) -> p f j d", d=FD)
                        nc.vector.tensor_tensor(dst, sums[:, :, :, 0:FD],
                                                    frec[:].unsqueeze(3).broadcast_to([P, GH, T, FD]), ALU.mult).then_inc(fnormed, 1)
                    elif kind == "attn":
                        dve.wait_ge(wk_full, now(b, wk_full, WK[x_]))
                        if x_[1]:
                            dve.wait_ge(misc_read, now(b, misc_read, MISC[x_] - 1))
                        nc.vector.tensor_tensor(y[:], wk_of(x_)[:].rearrange("p (t d) -> p t d", d=D), y[:],
                                                    ALU.add).then_inc(misc_read, 1)
                    elif kind == "wo":
                        dve.wait_ge(wk_full, now(b, wk_full, WK[x_]))
                        src = wk_of(x_)[:].rearrange("p (t d) -> p t d", d=D)
                        layernorm(b, lambda t: src[:, t])
                        for t in range(T):
                            ins = nc.vector.tensor_scalar(branch[:, t], src[:, t], moments[:, t, 0:1], rstd[:, t:t + 1],
                                                          ALU.subtract, ALU.mult)
                        ins.then_inc(misc_read, 1)
                        dve.wait_ge(misc_read, now(b, misc_read, MISC[x_]))
                        nc.vector.tensor_tensor(branch[:], branch[:],
                                                affine[:, 0].unsqueeze(1).broadcast_to([P, T, D]), ALU.mult).then_inc(step_done, 1)
                        dve.wait_ge(step_done, now(b, step_done, next_step()))
                        nc.vector.tensor_tensor(branch[:], branch[:],
                                                affine[:, 1].unsqueeze(1).broadcast_to([P, T, D]), ALU.add).then_inc(step_done, 1)
                        dve.wait_ge(step_done, now(b, step_done, next_step()))
                        nc.vector.tensor_tensor(x2[:], branch[:], xn[:], ALU.add).then_inc(x2_done, 1)
                    elif kind == "gate":
                        dve.wait_ge(misc_read, now(b, misc_read, MISC[("attn", BLOCKS - 1)]))
                        dve.wait_ge(x2_done, now(b, x2_done, 1))
                        nc.vector.tensor_tensor(y[:], y[:], x2[:], ALU.add).then_inc(step_done, 1)
                        dve.wait_ge(step_done, now(b, step_done, next_step()))
                        dve.wait_ge(wk_full, now(b, wk_full, WK[x_]))
                        src = wk_of(x_)[:, 0:T * E].rearrange("p (t e) -> p t e", e=E)
                        wide = [P, T, E]
                        nc.vector.tensor_reduce(gmax[:].unsqueeze(2), src, AX.X, ALU.max, negate=True).then_inc(step_done, 1)
                        dve.wait_ge(step_done, now(b, step_done, next_step()))
                        nc.vector.tensor_tensor(glog[:], src, gmax[:].unsqueeze(2).broadcast_to(wide), ALU.add).then_inc(step_done, 1)
                        dve.wait_ge(step_done, now(b, step_done, next_step()))
                        nc.vector.memset(gtop[:], 0.0).then_inc(misc_read, 1)
                        nc.vector.memset(gidx[:], 0).then_inc(logits, 1)
                        dve.wait_ge(gate_exp, now(b, gate_exp, 1))
                        nc.vector.tensor_reduce(gsum[:].unsqueeze(2), gexp[:], AX.X, ALU.add).then_inc(step_done, 1)
                        dve.wait_ge(step_done, now(b, step_done, next_step()))
                        nc.vector.reciprocal(grec[:], gsum[:]).then_inc(step_done, 1)
                        dve.wait_ge(step_done, now(b, step_done, next_step()))
                        nc.vector.tensor_tensor(gprob[:], gexp[:], grec[:].unsqueeze(2).broadcast_to(wide), ALU.mult).then_inc(step_done, 1)
                        dve.wait_ge(step_done, now(b, step_done, next_step()))
                        carry_wait()
                        for t in range(T):
                            ins = nc.vector.max(gtop[:, t], gprob[:, t])
                        ins.then_inc(step_done, 1)
                        dve.wait_ge(step_done, now(b, step_done, next_step()))
                        carry_wait()
                        for t in range(T):
                            ins = nc.vector.max_index(gidx[:, t], gtop[:, t], gprob[:, t])
                        ins.then_inc(step_done, 1)
                        dve.wait_ge(step_done, now(b, step_done, next_step()))
                        nc.vector.tensor_copy(gidf[:], gidx[:]).then_inc(step_done, 1)
                        dve.wait_ge(step_done, now(b, step_done, next_step()))
                        iota = experts.unsqueeze(1).broadcast_to(wide)
                        nc.vector.tensor_tensor(gate_a[:], iota, gidf[:, :, 0:1].broadcast_to(wide), ALU.is_equal).then_inc(step_done, 1)
                        dve.wait_ge(step_done, now(b, step_done, next_step()))
                        nc.vector.tensor_tensor(gate_b[:], iota, gidf[:, :, 1:2].broadcast_to(wide), ALU.is_equal).then_inc(step_done, 1)
                        dve.wait_ge(step_done, now(b, step_done, next_step()))
                        nc.vector.tensor_tensor(gate_a[:], gate_a[:], gtop[:, :, 0:1].broadcast_to(wide), ALU.mult).then_inc(step_done, 1)
                        dve.wait_ge(step_done, now(b, step_done, next_step()))
                        nc.vector.tensor_tensor(gate_b[:], gate_b[:], gtop[:, :, 1:2].broadcast_to(wide), ALU.mult).then_inc(step_done, 1)
                        dve.wait_ge(step_done, now(b, step_done, next_step()))
                        nc.vector.tensor_tensor(gate_w[:], gate_a[:], gate_b[:], ALU.add).then_inc(step_done, 1)
                        dve.wait_ge(step_done, now(b, step_done, next_step()))
                    elif kind == "moe":
                        _, t, half = x_
                        dve.wait_ge(wk_full, now(b, wk_full, WK[x_]))
                        e0 = half * HALF
                        nc.vector.tensor_tensor(
                            weighted[:, e0:e0 + HALF], wk_of(x_)[:].rearrange("p (e d) -> p e d", d=D),
                            gate_w[:, t, e0:e0 + HALF].unsqueeze(2).broadcast_to([P, HALF, D]), ALU.mult).then_inc(misc_read, 1)
                        if half == 1:
                            dve.wait_ge(misc_read, now(b, misc_read, MISC[x_]))
                            nc.vector.tensor_reduce(branch[:, t].unsqueeze(2), weighted.rearrange("p e d -> p d e"),
                                                    AX.X, ALU.add).then_inc(step_done, 1)
                            dve.wait_ge(step_done, now(b, step_done, next_step()))
                layernorm(b, lambda t: branch[:, t])
                for t in range(T):
                    ins = nc.vector.tensor_scalar(branch[:, t], branch[:, t], moments[:, t, 0:1], rstd[:, t:t + 1],
                                                  ALU.subtract, ALU.mult)
                ins.then_inc(step_done, 1)
                dve.wait_ge(step_done, now(b, step_done, next_step()))
                nc.vector.tensor_tensor(branch[:], branch[:],
                                        affine[:, 2].unsqueeze(1).broadcast_to([P, T, D]), ALU.mult).then_inc(step_done, 1)
                dve.wait_ge(step_done, now(b, step_done, next_step()))
                nc.vector.tensor_tensor(branch[:], branch[:],
                                        affine[:, 3].unsqueeze(1).broadcast_to([P, T, D]), ALU.add).then_inc(step_done, 1)
                dve.wait_ge(step_done, now(b, step_done, next_step()))
                dve.wait_ge(out_sent, b * 16 + 16)
                nc.vector.tensor_tensor(result[:], branch[:], y[:], ALU.add).then_inc(result_done, 1)
                assert taken[0] == N_STEP, taken

        @block.tensor
        def _(pe):
            start(pe, wk_full, sm_full, st_full, pv_full, fpv_full)
            pe.sem_inc(out_sent, 16)
            pe.wait_ge(prepared, 6)

            def split3(dst, lh, ll, rh, rl, bias=None, first=True):
                nc.tensor.matmul(dst, lh, rh, start=first, stop=False)
                nc.tensor.matmul(dst, ll, rh, start=False, stop=False)
                ins = nc.tensor.matmul(dst, lh, rl, start=False, stop=bias is None)
                if bias is not None:
                    ins = nc.tensor.matmul(dst, bias[0], bias[1], start=False, stop=True)
                return ins

            def bias_rows(name, a=0, n=None):
                p0, at, whole = BIAS[name]
                return biases[p0:p0 + 2, at + a:at + a + (n or whole)]

            def one_rows(name):
                return biases[BIAS[name][0]:BIAS[name][0] + 2, ONES:ONES + P]

            with pe.Fori(0, B) as b:
                for x_ in PLAN:
                    kind = x_[0]
                    if x_ in WK:
                        n = WK[x_]
                        read, c = wk_freed(WK_LIST[n - 3])
                        pe.wait_ge(read, now(b, read, c) if n >= 3 else past(b, read, c))
                        bank = wk_of(x_)
                    if kind == "xT":
                        pe.wait_ge(normal, now(b, normal, 1))
                        for t in range(T):
                            ins = nc.tensor.transpose(bank[:, t * P:(t + 1) * P], xn[:, t], ident)
                        ins.then_inc(wk_full, 1)
                    elif kind == "v":
                        _, t, half = x_
                        pe.wait_ge(split, now(b, split, SPLIT[("xT",)]))
                        a = 2 * H * DH + half * 512
                        tok = slice(t * P, (t + 1) * P)
                        split3(bank[:], xt_h[:, tok], xt_l[:, tok], wqkv_h[:, a:a + 512], wqkv_l[:, a:a + 512]).then_inc(wk_full, 1)
                    elif kind == "fv":
                        pe.wait_ge(split, now(b, split, SPLIT[("xT",)]))
                        for t in range(T):
                            tok = slice(t * P, (t + 1) * P)
                            ins = split3(bank[:, tok], xt_h[:, tok], xt_l[:, tok], small_h[:, 0:D], small_l[:, 0:D],
                                         (one_rows("bv"), bias_rows("bv")))
                        ins.then_inc(wk_full, 1)
                    elif kind in ("fq", "fk"):
                        g, n = x_[1], int(kind == "fk")
                        pe.wait_ge(split, now(b, split, SPLIT[("xT",)]))
                        wh = strips_h[:, n, g * GH:(g + 1) * GH].rearrange("p h c -> p (h c)")
                        wl = strips_l[:, n, g * GH:(g + 1) * GH].rearrange("p h c -> p (h c)")
                        name = "bk" if n else "bq"
                        split3(bank[:], wh, wl, xt_h[:], xt_l[:], (bias_rows(name, g * P, P), biases[BIAS[name][0]:BIAS[name][0] + 2, S:2 * S])).then_inc(wk_full, 1)
                    elif kind == "proj":
                        _, g, pair = x_
                        pe.wait_ge(split, now(b, split, SPLIT[("xT",)]))
                        n = PH * DH
                        for t in range(2 * pair, 2 * pair + 2):
                            tok = slice(t * P, (t + 1) * P)
                            for k in range(2):
                                a, at = k * H * DH + g * n, (t % 2 * 2 + k) * n
                                ins = split3(bank[:, at:at + n], xt_h[:, tok], xt_l[:, tok],
                                             wqkv_h[:, a:a + n], wqkv_l[:, a:a + n])
                        ins.then_inc(wk_full, 1)
                    elif kind in ("tq", "tk"):
                        h = x_[1]
                        g, k = h // PH, int(kind == "tk")
                        if h % PH == 0:
                            pe.wait_ge(rotated, now(b, rotated, 2 * PROJ[("proj", g, 1)]))
                        for t in range(T):
                            src = qk[:, g % 2, t, k * PH + h % PH].rearrange("p r d -> p (r d)")
                            ins = nc.tensor.transpose(bank[:, t * P:(t + 1) * P], src, ident)
                        ins.then_inc(wk_full, 1)
                    elif kind == "mT":
                        h = x_[1]
                        pe.wait_ge(max_done, now(b, max_done, SM[("sm", h, 2)]))
                        for t in range(T):
                            src = nmax[:, h % 4, t:t + 1].broadcast_to([P, DH + 1])
                            ins = nc.tensor.transpose(bank[0:DH + 1, t * P:(t + 1) * P], src, ident)
                        ins.then_inc(wk_full, 1)
                    elif kind == "fmT":
                        g = x_[1]
                        pe.wait_ge(max_done, now(b, max_done, SM[("fsm", GH * g + GH - 1, T - 1)]))
                        for t in range(T):
                            src = fnmax[:, t].rearrange("p h c -> p (h c)")
                            ins = nc.tensor.transpose(bank[:, t * P:(t + 1) * P], src, ident)
                        ins.then_inc(wk_full, 1)
                    elif kind == "sm":
                        _, h, u = x_
                        if u == 0:
                            pe.wait_ge(split, now(b, split, SPLIT[("tk", h)]))
                        pe.wait_ge(max_done, since(b, max_done, SM[x_] - 2))
                        bank = sm_bank[(SM[x_] - 1) % 2]
                        for j, at in SM_UNITS[u]:
                            nc.tensor.matmul(bank[:, at:at + (j + 1) * P], q_hl[:, h % 4, j * P:(j + 1) * P],
                                             k_hh[:, h % 4, 0:(j + 1) * P], start=True, stop=True)
                            ins = nc.tensor.matmul(bank[:, at + j * P:at + (j + 1) * P], masks[:, 0], masks[:, 1],
                                                   start=False, stop=True, skip_group_check=True)
                        ins.then_inc(sm_full, 1)
                    elif kind == "fsm":
                        _, f, j = x_
                        g, r = f // GH, slice(f % GH * STRIP, (f % GH + 1) * STRIP)
                        pe.wait_ge(split, now(b, split, max(SPLIT[("fq", g)], SPLIT[("fk", g)])))
                        pe.wait_ge(max_done, since(b, max_done, SM[x_] - 2))
                        bank = sm_bank[(SM[x_] - 1) % 2]
                        nc.tensor.matmul(bank[:], fq[r, g % 3, j * P:(j + 1) * P], fk[r, g % 3], start=True, stop=True,
                                             tile_position=(r.start, 0)).then_inc(sm_full, 1)
                    elif kind == "st":
                        _, h, u = x_
                        if u == 0:
                            pe.wait_ge(max_row_done, now(b, max_row_done, h + 1))
                        pe.wait_ge(exp_done, since(b, exp_done, ST[x_] - 2))
                        bank = st_bank[(ST[x_] - 1) % 2]
                        for i, at in ST_UNITS[u]:
                            dst = bank[:, at:at + S - i * P]
                            nc.tensor.matmul(dst, k_hh[:, h % 4, i * P:(i + 1) * P], q_hl[:, h % 4, i * P:S],
                                             start=True, stop=False)
                            nc.tensor.matmul(dst, k_l1[0:DH + 1, h % 4, i * P:(i + 1) * P], q_hm[0:DH + 1, h % 4, i * P:S],
                                             start=False, stop=True)
                            ins = nc.tensor.matmul(bank[:, at:at + P], masks[:, 0], masks[:, 2],
                                                   start=False, stop=True, skip_group_check=True)
                        ins.then_inc(st_full, 1)
                    elif kind == "fst":
                        _, f, i = x_
                        g, r = f // GH, slice(f % GH * STRIP, (f % GH + 1) * STRIP)
                        pe.wait_ge(fmax_done, now(b, fmax_done, g + 1))
                        pe.wait_ge(exp_done, since(b, exp_done, ST[x_] - 2))
                        bank = st_bank[(ST[x_] - 1) % 2]
                        nc.tensor.matmul(bank[:], fk[r, g % 3, i * P:(i + 1) * P], fq[r, g % 3], start=True, stop=True,
                                             tile_position=(r.start, 0)).then_inc(st_full, 1)
                    elif kind == "pv":
                        _, h, j = x_
                        if j == 0:
                            pe.wait_ge(exp_done, now(b, exp_done, ST[("st", h, 2)]))
                            pe.wait_ge(normed, since(b, normed, h))
                            if h == 0:
                                pe.wait_ge(v_act, now(b, v_act, len(V_ACT)))
                                pe.wait_ge(v_dve, now(b, v_dve, len(V_DVE)))
                        for i in range(j + 1):
                            a = PT_AT[i] + (j - i) * P
                            ins = nc.tensor.matmul(pv_bank[:, j * VW:(j + 1) * VW], pt[:, h % 2, a:a + P], v[:, i, h],
                                                   start=(i == 0), stop=(i == j))
                        if j == T - 1:
                            ins.then_inc(pv_full, 1)
                    elif kind == "fpv":
                        _, f, j = x_
                        if j == 0:
                            pe.wait_ge(exp_done, now(b, exp_done, ST[("fst", f, T - 1)]))
                            if f % GH == 0:
                                pe.wait_ge(fnormed, since(b, fnormed, f // GH))
                            if f == 0:
                                pe.wait_ge(v_dve, now(b, v_dve, V_DVE[("fv",)]))
                        a = (f % GH * T + j) * FVW
                        for i in range(T):
                            ins = nc.tensor.matmul(fpv_bank[:, a:a + FVW], fpt[:, f % 2, i, j * P:(j + 1) * P], fv[:, i, f],
                                                   start=(i == 0), stop=(i == T - 1))
                        if j == T - 1:
                            ins.then_inc(fpv_full, 1)
                    elif kind == "oT":
                        c = x_[1]
                        pe.wait_ge(normed, now(b, normed, 2 * c + 2))
                        for t in range(T):
                            ins = nc.tensor.transpose(bank[:, t * P:(t + 1) * P], o[:, t, c % 4], ident)
                        ins.then_inc(wk_full, 1)
                    elif kind == "attn":
                        c = x_[1]
                        pe.wait_ge(split, now(b, split, SPLIT[("oT", c)]))
                        for t in range(T):
                            tok = slice(t * P, (t + 1) * P)
                            ins = split3(bank[:, tok], ot_h[:, c % 2, tok], ot_l[:, c % 2, tok], wout_h[:, c], wout_l[:, c])
                        ins.then_inc(wk_full, 1)
                    elif kind == "cT":
                        pe.wait_ge(fnormed, now(b, fnormed, G))
                        for t in range(T):
                            ins = nc.tensor.transpose(bank[:, t * P:(t + 1) * P], ct[:, t], ident)
                        ins.then_inc(wk_full, 1)
                    elif kind == "wo":
                        pe.wait_ge(split, now(b, split, SPLIT[("cT",)]))
                        for t in range(T):
                            tok = slice(t * P, (t + 1) * P)
                            ins = split3(bank[:, tok], ct_h[:, tok], ct_l[:, tok], small_h[:, D:2 * D], small_l[:, D:2 * D],
                                         (one_rows("bo"), bias_rows("bo")))
                        ins.then_inc(wk_full, 1)
                    elif kind == "x2T":
                        pe.wait_ge(x2_done, now(b, x2_done, 1))
                        for t in range(T):
                            ins = nc.tensor.transpose(bank[:, t * P:(t + 1) * P], x2[:, t], ident)
                        ins.then_inc(wk_full, 1)
                    elif kind == "gate":
                        pe.wait_ge(split, now(b, split, SPLIT[("x2T",)]))
                        for t in range(T):
                            tok = slice(t * P, (t + 1) * P)
                            ins = split3(bank[:, t * E:(t + 1) * E], x2t_h[:, tok], x2t_l[:, tok],
                                         small_h[:, 2 * D:2 * D + E], small_l[:, 2 * D:2 * D + E],
                                         (one_rows("bg"), bias_rows("bg")))
                        ins.then_inc(wk_full, 1)
                    elif kind == "moe":
                        _, t, half = x_
                        tok = slice(t * P, (t + 1) * P)
                        e = slice(half * HALF, (half + 1) * HALF)
                        split3(bank[:], x2t_h[:, tok], x2t_l[:, tok], we_h[:, e].rearrange("p e d -> p (e d)"),
                                   we_l[:, e].rearrange("p e d -> p (e d)"),
                                   (one_rows("bexp"), bias_rows("bexp", half * 512, 512))).then_inc(wk_full, 1)


_INS = ["L0_attn_x", "L0_attn_W_qkv", "L0_attn_W_out", "L0_ffn_Wq", "L0_ffn_bq", "L0_ffn_Wk", "L0_ffn_bk", "L0_ffn_Wv",
        "L0_ffn_bv", "L0_ffn_Wo", "L0_ffn_bo", "L0_ffn_g1", "L0_ffn_be1", "L0_ffn_g2", "L0_ffn_be2", "L0_ffn_Wg",
        "L0_ffn_bg", "L0_ffn_We", "L0_ffn_bexp"]


def _tables():
    import numpy as np

    table = np.zeros((P, C_N), np.float32)
    p, n = np.arange(P)[:, None], np.arange(P)[None, :]
    table[:, C_ID:C_ID + P] = p == n
    table[:, C_MS:C_MS + P] = np.where(n > p, -1e30, 0)
    table[:, C_MT:C_MT + P] = np.where(p > n, -1e30, 0)
    row = np.arange(P) % STRIP
    table[:, C_COL] = np.where(np.arange(P) >= DH, -1, 0)
    table[:, C_COL + 1] = np.where((row >= 2 * FD) & (row < 3 * FD), -1, 0)
    table[:, C_COL + 2] = np.where(row >= 3 * FD, -1, 0)
    table[:, C_COL + 3] = np.where(row == 1, -1, 0)
    table[:, C_IOTA:C_IOTA + E] = np.arange(E)
    pairs = np.arange(0, DH, 2).astype(np.float32)
    freqs = (np.float32(1.0) / np.float32(10000.0) ** (pairs / np.float32(DH))).astype(np.float32)
    angle = (np.arange(S).astype(np.float32)[:, None] * freqs[None, :]).astype(np.float32)
    sines = np.stack([np.sin(angle), -np.sin(angle)], 2).reshape(S, DH)
    rope = np.concatenate([np.cos(angle), sines], 1).astype(np.float32)
    return table, rope


def kernel(**inputs):
    import numpy as _np
    import concourse.bacc as _bacc
    from concourse import mybir as _mybir
    from concourse.bass_utils import run_bass_kernel_spmd as _run

    nc = _bacc.Bacc("TRN2", target_bir_lowering=False, num_devices=1)
    table, rope = _tables()
    given = {name: _np.ascontiguousarray(inputs[name]) for name in _INS}
    given["table"], given["rope"] = table, rope
    arrays, args = {}, []
    for name, a in given.items():
        arrays[f"in_{name}_dram"] = a
        args.append(nc.dram_tensor(f"in_{name}_dram", a.shape, _mybir.dt.from_np(a.dtype), kind="ExternalInput").ap())
    args.append(nc.dram_tensor("out_0_dram", (B, S, D), _mybir.dt.float32, kind="ExternalOutput").ap())
    build(nc, *args)
    r = _run(nc, [arrays], core_ids=[0])
    return r.results[0]["out_0_dram"]
```

```python
import concourse.bass as bass
from concourse import mybir
from contextlib import ExitStack
import math

F32 = mybir.dt.float32
F32R = mybir.dt.float32r
BF16 = mybir.dt.bfloat16
U32 = mybir.dt.uint32
ALU = mybir.AluOpType
ACT = mybir.ActivationFunctionType
AX = mybir.AxisListType

B, S, D = 8, 512, 128
P = 128
T = S // P
H, DH = 16, 64
FH, FD = 16, 8
PH = 2
PG = H // PH
GH = 4
G = FH // GH
E = 8
STRIP = 32
EPS = 1e-5
FVW = FD + 1
HALF = 512 // D

BIAS = {"bexp": (0, 0, E * D), "bq": (32, 0, FH * STRIP), "bk": (64, 0, FH * STRIP),
        "bv": (96, 0, D), "bo": (96, D, D), "bg": (96, 2 * D, E)}
ONES = E * D
BIAS_N = ONES + P

C_ID, C_COL, C_IOTA = 0, P, P + 4
C_N = C_IOTA + E
C_MS, C_MT = C_N, C_N + P

SM_UNITS = [[(3, 0)], [(2, 0), (0, 3 * P)], [(1, 0)]]
ST_UNITS = [[(0, 0)], [(1, 0), (3, 3 * P)], [(2, 0)]]
ST_N = [S, S, 2 * P]
PT_AT = [0, S, 2 * S, S + 3 * P]


def body_plan():
    plan = []
    for s in range(H + 7):
        st, wk, sm, pv = [], [], [], []
        g = s // 2
        if s % 2 == 0 and g < G:
            wk.append(("fmT", g))
        if 0 <= s - 2 < H:
            wk.append(("mT", s - 2))
        if s < H:
            wk += [("tq", s), ("tk", s)]
        if s // PH + 1 < PG:
            wk.append(("proj", s // PH + 1, s % PH))
        if s in (0, 3):
            wk += [("fq", 2 + s // 3), ("fk", 2 + s // 3)]
        if s == 0:
            wk.append(("fv",))
        if s >= 4 and s % 2 == 0 and (s - 4) // 2 < G:
            wk.append(("fT", (s - 4) // 2))
        if 1 <= s <= 4:
            wk += [("v", s - 1, half) for half in range(2)]
        wk += {11: [("cT",)], 12: [("wo",)], 14: [("x2T",)], 15: [("gate",)], 16: [("pick",)]}.get(s, [])
        if 16 <= s < 16 + T:
            wk += [("moe", s - 16, half) for half in range(2)]
        if s == 21:
            wk.append(("norm",))
        if s >= 8 and s % 2 == 0 and (s - 8) // 2 < PG:
            wk.append(("attn", (s - 8) // 2))
        if 0 <= s - 1 < H:
            sm += [("sm", s - 1, u) for u in range(3)]
        if g + 1 < G:
            sm += [("fsm", (g + 1) * GH + f, j) for f in range(s % 2 * 2, s % 2 * 2 + 2) for j in range(T)]
        if 0 <= s - 3 < H:
            st += [("st", s - 3, u) for u in range(3)]
        for m in range(2 * s - 2, 2 * s):
            if 0 <= m < G * T:
                st += [("fst", m // T, m % T, f) for f in range(GH)]
            if 1 <= m <= G * T:
                st.append(("fpv", (m - 1) // T, (m - 1) % T))
        if s >= 5 and s % 2 == 1 and (s - 5) // 2 < PG:
            pv += [("pv", (s - 5) // 2, i) for i in range(T)]
        if s == 17:
            wk.append(("ln",))
        if s == 18:
            wk += [("xT",), ("proj", 0, 0), ("proj", 0, 1), ("fq", 0), ("fk", 0)]
        if s == 19:
            wk += [("fq", 1), ("fk", 1)]
        if 19 <= s < 19 + GH:
            sm += [("fsm", s - 19, j) for j in range(T)]
        lists = [st, wk, sm, pv]
        most = max(map(len, lists))
        for k in range(most):
            for x in lists:
                plan += x[k * len(x) // most:(k + 1) * len(x) // most]
    return plan


PLAN = body_plan()
OPENING = [x for x in PLAN if x in (("ln",), ("xT",)) or x[0:2] in (("proj", 0), ("fq", 0), ("fk", 0), ("fq", 1), ("fk", 1))
           or (x[0] == "fsm" and x[1] < GH)]
WK_KINDS = ("xT", "v", "fv", "fq", "fk", "proj", "tq", "tk", "sm", "fsm", "mT", "fmT", "fT", "attn", "cT", "wo", "x2T",
            "gate", "moe")
SPLIT_KINDS = ("xT", "fq", "fk", "tq", "tk", "cT", "x2T")


def numbered(choose):
    return {x: n + 1 for n, x in enumerate(x for x in PLAN if choose(x))}


WK_LIST = [x for x in PLAN if x[0] in WK_KINDS]
WK_AT = {x: n for n, x in enumerate(WK_LIST)}
WK_BANKS = 3
assert len(WK_LIST) % WK_BANKS == 0, len(WK_LIST)
FULL = numbered(lambda x: x in WK_AT and x not in OPENING)
OPEN_FULL = numbered(lambda x: x in WK_AT and x in OPENING)
MAX = numbered(lambda x: x[0] in ("sm", "fsm"))
ST = numbered(lambda x: x[0] in ("st", "fst"))
SPLIT = numbered(lambda x: x[0] in SPLIT_KINDS and x not in OPENING)
OPEN_SPLIT = numbered(lambda x: x[0] in SPLIT_KINDS and x in OPENING)
PROJ = numbered(lambda x: x[0] == "proj")
V_ACT = numbered(lambda x: x[0] == "v" and x[2] == 0)
V_DVE = numbered(lambda x: x[0] == "fv" or (x[0] == "v" and x[2] == 1))
MISC = numbered(lambda x: x[0] in ("attn", "wo", "gate", "moe"))
N_STEP = 38
N_OPEN_STEP = 2


def build(nc, x, w_qkv, w_out, wq, bq, wk, bk, wv, bv, wo, bo, g1, be1, g2, be2, wg, bg, we, bexp, table, rope, out):
    with ExitStack() as ctx:
        def sb(name, shape, dt=F32):
            return ctx.enter_context(nc.sbuf_tensor(name, shape, dt))

        def sem(name):
            return ctx.enter_context(nc.semaphore(name))

        consts = sb("consts", [P, C_N])
        ident = consts[:, C_ID:C_ID + P]
        low_rows = consts[:, C_COL:C_COL + 1]
        q_low = consts[:, C_COL + 1:C_COL + 2]
        k_low = consts[:, C_COL + 2:C_COL + 3]
        second = consts[:, C_COL + 3:C_COL + 4]
        experts = consts[:, C_IOTA:C_IOTA + E]
        masks = sb("masks", [P, 3, P], BF16)
        angles = sb("angles", [P, T, 3 * DH // 2])
        wqkv_h = sb("wqkv_h", [P, 3 * H * DH], F32R)
        wqkv_l = sb("wqkv_l", [P, 3 * H * DH], F32R)
        wout_h = sb("wout_h", [P, PG, D], F32R)
        wout_l = sb("wout_l", [P, PG, D], F32R)
        we_h = sb("we_h", [P, E, D], F32R)
        we_l = sb("we_l", [P, E, D], F32R)
        small_h = sb("small_h", [P, 2 * D + E], F32R)
        small_l = sb("small_l", [P, 2 * D + E], F32R)
        strips_h = sb("strips_h", [P, 2, FH, STRIP], F32R)
        strips_l = sb("strips_l", [P, 2, FH, STRIP], F32R)
        affine = sb("affine", [P, 4, D])
        biases = sb("biases", [P, BIAS_N], F32R)

        x_in = sb("x_in", [P, T, D])
        xn = sb("xn", [P, T, D])
        xt_h = sb("xt_h", [P, S], F32R)
        xt_l = sb("xt_l", [P, S], F32R)
        v = sb("v", [P, T, H, DH])
        ones = sb("ones", [P, DH])
        fv = sb("fv", [P, T, FH, FVW])
        rot = sb("rot", [P, 2, 2, 2 * PH * DH])
        qk = sb("qk", [P, 2, T, 2 * PH, 2, DH])
        q_hl = sb("q_hl", [P, 4, S], F32R)
        q_hm = sb("q_hm", [P, 4, S], F32R)
        k_hh = sb("k_hh", [P, 4, S], F32R)
        k_l1 = sb("k_l1", [P, 4, S], F32R)
        fq = sb("fq", [P, 3, S], F32R)
        fk = sb("fk", [P, 3, S], F32R)
        nmax = sb("nmax", [P, 4, T])
        fnmax = sb("fnmax", [P, T, GH, STRIP])
        pt = sb("pt", [P, 3, 2 * S + 2 * P])
        fpt = sb("fpt", [P, 2, GH, S])
        fo = sb("fo", [P, S])
        frec = sb("frec", [P, T, GH])
        u = sb("u", [P, S])
        u_h = sb("u_h", [P, 2, S], F32R)
        u_l = sb("u_l", [P, 2, S], F32R)
        ct = sb("ct", [P, T, D])
        ct_h = sb("ct_h", [P, S], F32R)
        ct_l = sb("ct_l", [P, S], F32R)
        x2 = xn
        x2t_h, x2t_l = ct_h, ct_l
        y = sb("y", [P, T, D])
        branch = ct
        weighted = sb("weighted", [P, E, D])
        stats = sb("stats", [P, T, 6])
        moments = sb("moments", [P, T, 2])
        spread = sb("spread", [P, T])
        rstd = sb("rstd", [P, T])
        spread_x = sb("spread_x", [P, T])
        rstd_x = sb("rstd_x", [P, T])
        power = sb("power", [P, T])
        spare = sb("spare", [P, 1])
        early = weighted[:].rearrange("p e d -> p (e d)")[:, 0:7 * T * E].rearrange("p (a t e) -> p a t e", a=7, e=E)
        gmax = sb("gmax", [P, T])
        gsum = sb("gsum", [P, T])
        grec = sb("grec", [P, T])
        glog = early[:, 4]
        gexp = early[:, 5]
        gprob = early[:, 0]
        gtop = sb("gtop", [P, T, E])
        gidx = early[:, 6].bitcast(U32)
        gidf = early[:, 1]
        gate_a = early[:, 2]
        gate_b = early[:, 3]
        gate_w = sb("gate_w", [P, T, E])
        qk_flat = qk[:].rearrange("p a t h r d -> p (a t h r d)")
        rot_flat = rot[:].rearrange("p a c n -> p (a c n)")
        raw_qkv = fpt[:].rearrange("p a t n -> p (a t n)")[:, 0:3 * H * DH]
        raw_out = qk_flat[:, 0:PG * D].rearrange("p (c n) -> p c n", n=D)
        raw_we = qk_flat[:, PG * D:PG * D + E * D].rearrange("p (e n) -> p e n", n=D)
        raw_masks = qk_flat[:, (PG + E) * D:(PG + E + 2) * D].rearrange("p (c n) -> p c n", n=P)
        raw_small = rot_flat[:, 0:2 * D + E]
        raw_qk = rot_flat[:, 512:512 + 2 * D]
        raw_bias = pt[:].rearrange("p a n -> p (a n)")[:, 0:BIAS_N]
        hi_bias = v[:].rearrange("p t h d -> p (t h d)")[:, 0:BIAS_N].bitcast(F32R)

        wk_bank = [ctx.enter_context(nc.psum_tensor(f"wk{i}", [P, 512], F32)) for i in range(WK_BANKS)]
        st_bank = [ctx.enter_context(nc.psum_tensor(f"st{i}", [P, 512], F32)) for i in range(2)]
        o_bank = ctx.enter_context(nc.psum_tensor("o_bank", [P, 512], F32))
        l_bank = ctx.enter_context(nc.psum_tensor("l_bank", [P, 512], F32))
        f_bank = ctx.enter_context(nc.psum_tensor("f_bank", [P, 512], F32))

        loaded = sem("loaded")
        x_loaded = sem("x_loaded")
        out_sent = sem("out_sent")
        prepared = sem("prepared")
        prep_pool = sem("prep_pool")
        prep_dve = sem("prep_dve")
        events, before = {}, {}

        def per_turn(name, n, opening=0):
            s = sem(name)
            events[id(s)], before[id(s)] = n, n - opening
            return s

        wk_full = per_turn("wk_full", len(FULL))
        open_full = per_turn("open_full", len(OPEN_FULL), len(OPEN_FULL))
        st_full = per_turn("st_full", len(ST))
        o_full = per_turn("o_full", PG)
        f_summed = per_turn("f_summed", G * T)
        rounded = per_turn("rounded", len(SPLIT))
        open_rounded = per_turn("open_rounded", len(OPEN_SPLIT), len(OPEN_SPLIT))
        v_act = per_turn("v_act", len(V_ACT))
        row_done = per_turn("row_done", H)
        exp_done = per_turn("exp_done", len(ST))
        fo_done = per_turn("fo_done", G)
        u_rounded = per_turn("u_rounded", PG)
        gate_exp = per_turn("gate_exp", 1)
        split = per_turn("split", len(SPLIT))
        open_split = per_turn("open_split", len(OPEN_SPLIT), len(OPEN_SPLIT))
        v_dve = per_turn("v_dve", len(V_DVE))
        turned = per_turn("turned", 2 * len(PROJ), 4)
        rotated = per_turn("rotated", 2 * len(PROJ), 4)
        x_variance = per_turn("x_variance", 1, 1)
        x_rstd = per_turn("x_rstd", 1, 1)
        variance = per_turn("variance", 2)
        rstd_done = per_turn("rstd_done", 2)
        max_done = per_turn("max_done", len(MAX), GH * T)
        fmax_done = per_turn("fmax_done", G)
        divided = per_turn("divided", PG)
        u_split = per_turn("u_split", PG)
        fdivided = per_turn("fdivided", G)
        misc_read = per_turn("misc_read", len(MISC))
        normal = per_turn("normal", 1, 1)
        x2_done = per_turn("x2_done", 1)
        logits = per_turn("logits", 1)
        step_done = per_turn("step_done", N_STEP)
        open_step = per_turn("open_step", N_OPEN_STEP, N_OPEN_STEP)

        def now(b, s, c):
            assert 1 <= c <= events[id(s)], (c, events[id(s)])
            return b * events[id(s)] + (events[id(s)] + c)

        def past(b, s, c):
            assert 1 <= c <= events[id(s)], (c, events[id(s)])
            return b * events[id(s)] + c

        def since(b, s, c, wrap):
            return past(b, s, c) if wrap else now(b, s, c)

        def start(eng, *sems):
            for s in sems:
                if before[id(s)]:
                    eng.sem_inc(s, before[id(s)])

        def wk_of(x):
            return wk_bank[WK_AT[x] % WK_BANKS]

        def full_of(x):
            return (open_full, OPEN_FULL[x]) if x in OPEN_FULL else (wk_full, FULL[x])

        def split_of(x):
            return (open_split, OPEN_SPLIT[x]) if x in OPEN_SPLIT else (split, SPLIT[x])

        def bank_read(x):
            if x[0] in SPLIT_KINDS:
                return split_of(x)
            if x in V_ACT:
                return v_act, V_ACT[x]
            if x in V_DVE:
                return v_dve, V_DVE[x]
            if x in MAX:
                return max_done, MAX[x]
            return {"proj": lambda: (turned, 2 * PROJ[x]), "mT": lambda: (row_done, x[1] + 1),
                    "fmT": lambda: (fmax_done, x[1] + 1), "fT": lambda: (fdivided, x[1] + 1)
                    }.get(x[0], lambda: (misc_read, MISC[x]))()

        x_tiles = x.rearrange("b (t p) d -> b p t d", p=P)
        out_tiles = out.rearrange("b (t p) d -> b p t d", p=P)
        N_LOADS = 15 + 2 * (4 + 6)

        block = ctx.enter_context(nc.Block())

        @block.sync
        def _(sp):
            sp.dma_start(x_in[:], x_tiles[0]).then_inc(x_loaded, 16)
            loads = [
                (raw_qkv, w_qkv), (consts[:], table[:, 0:C_N]),
                (raw_masks, table[:, C_MS:C_MS + 2 * P].rearrange("p (c n) -> p c n", n=P)), (angles[:], rope.rearrange("(t p) c -> p t c", p=P)),
                (raw_small[:, 0:D], wv), (raw_small[:, D:2 * D], wo), (raw_small[:, 2 * D:2 * D + E], wg),
                (raw_qk[:, 0:D], wq), (raw_qk[:, D:2 * D], wk),
                (raw_we, we.rearrange("e d f -> d e f")), (raw_out, w_out.rearrange("(c p) n -> p c n", p=P)),
            ]
            for n, a in enumerate((g1, be1, g2, be2)):
                loads.append((affine[:, n, :], a.rearrange("(a d) -> a d", a=1).broadcast_to([P, D])))
            for r in range(2):
                for name, a in (("bv", bv), ("bo", bo), ("bg", bg), ("bexp", bexp.rearrange("e d -> (e d)"))):
                    p0, at, n = BIAS[name]
                    loads.append((raw_bias[p0 + r:p0 + r + 1, at:at + n], a.rearrange("(a d) -> a d", a=1)))
                for name, a in (("bq", bq), ("bk", bk)):
                    p0, at, n = BIAS[name]
                    strip = raw_bias[p0 + r:p0 + r + 1, at:at + n].rearrange("p (h c) -> p h c", c=STRIP)
                    for c in range(1, 4):
                        loads.append((strip[:, :, c * FD:(c + 1) * FD], a.rearrange("(a h d) -> a h d", a=1, d=FD)))
            sp.wait_ge(prepared, 1)
            for dst, src in loads:
                sp.dma_start(dst, src).then_inc(loaded, 16)
            assert len(loads) == N_LOADS
            with sp.Fori(0, B - 1) as b:
                sp.wait_ge(misc_read, now(b, misc_read, MISC[("attn", 0)]))
                sp.dma_start(x_in[:], x_tiles[bass.ds(b + 1, 1)].rearrange("b p t d -> p (b t) d")).then_inc(x_loaded, 16)
                sp.wait_ge(misc_read, now(b, misc_read, MISC[("attn", PG - 1)]))
                sp.dma_start(out_tiles[bass.ds(b, 1)].rearrange("b p t d -> p (b t) d"), y[:]).then_inc(out_sent, 16)
            sp.wait_ge(misc_read, now(B - 1, misc_read, MISC[("attn", 0)]))
            sp.dma_start(x_in[:], x_tiles[B - 1]).then_inc(x_loaded, 16)
            sp.wait_ge(misc_read, now(B - 1, misc_read, MISC[("attn", PG - 1)]))
            sp.dma_start(out_tiles[B - 1], y[:]).then_inc(out_sent, 16)
            sp.wait_ge(out_sent, 16 * (B + 1))

        @block.gpsimd
        def _(pool):
            nc.gpsimd.memset(power[:], -0.5).then_inc(prep_pool, 1)
            pool.wait_ge(prep_pool, 1)
            start(pool, rotated, rstd_done, u_split)

            def step(b, x_):
                kind = x_[0]
                if kind == "proj":
                    _, g, pair = x_
                    for k in range(2):
                        t, n = 2 * pair + k, 2 * PROJ[x_] - 1 + k
                        pool.wait_ge(turned, now(b, turned, n))
                        if t == 0:
                            old = ("tk", PH * ((g - 2) % PG) + PH - 1)
                            pool.wait_ge(wk_full, since(b, wk_full, FULL[old], g == 1))
                        shape = [P, 2 * PH, 2, DH // 2]
                        c, s_ = (rot[:, n % 2, m].rearrange("p (h i two) -> p h i two", two=2, i=DH // 2) for m in range(2))
                        dst = qk[:, g % 2, t].rearrange("p h r (two i) -> p h r two i", two=2)
                        nc.gpsimd.tensor_tensor(
                            dst[:, :, :, 0], c[:, :, :, 0].unsqueeze(2).broadcast_to(shape),
                            s_[:, :, :, 1].unsqueeze(2).broadcast_to(shape), ALU.add)
                        nc.gpsimd.tensor_tensor(
                            dst[:, :, :, 1], c[:, :, :, 1].unsqueeze(2).broadcast_to(shape),
                            s_[:, :, :, 0].unsqueeze(2).broadcast_to(shape), ALU.add).then_inc(rotated, 1)
                elif kind == "pv" and x_[2] == T - 1:
                    c = x_[1]
                    pool.wait_ge(u_rounded, now(b, u_rounded, c + 1))
                    nc.gpsimd.tensor_tensor(u_l[:, c % 2], u[:], u_h[:, c % 2].bitcast(F32), ALU.subtract)\
                        .then_inc(u_split, 1)
                elif kind == "ln":
                    pool.wait_ge(x_variance, now(b, x_variance, 1))
                    nc.gpsimd.tensor_tensor(rstd_x[:], spread_x[:], power[:], ALU.pow).then_inc(x_rstd, 1)
                elif kind in ("wo", "norm"):
                    n = 1 if kind == "wo" else 2
                    pool.wait_ge(variance, now(b, variance, n))
                    nc.gpsimd.tensor_tensor(rstd[:], spread[:], power[:], ALU.pow).then_inc(rstd_done, 1)

            for x_ in OPENING:
                step(-1, x_)
            with pool.Fori(0, B) as b:
                for x_ in PLAN:
                    step(b, x_)

        @block.scalar
        def _(act):
            act.wait_ge(loaded, 16 * N_LOADS)
            nc.scalar.copy(wqkv_h[:], raw_qkv).then_inc(prepared, 1)
            nc.scalar.copy(wout_h[:], raw_out).then_inc(prepared, 1)
            nc.scalar.copy(we_h[:], raw_we).then_inc(prepared, 1)
            nc.scalar.copy(small_h[:], raw_small).then_inc(prepared, 1)
            start(act, rounded, v_act, row_done, exp_done, fo_done, u_rounded, gate_exp)

            def step(b, x_):
                kind = x_[0]
                if kind in SPLIT_KINDS:
                    full, n = full_of(x_)
                    act.wait_ge(full, now(b, full, n))
                    src = wk_of(x_)[:]
                    if kind == "xT":
                        act.wait_ge(wk_full, now(b, wk_full, max(FULL[("fk", G - 1)], FULL[("proj", PG - 1, 1)],
                                                                 FULL[("v", T - 1, 1)])))
                        dst = xt_h[:]
                    elif kind in ("fq", "fk"):
                        g = x_[1]
                        user = {0: 3, 1: 1, 2: 2, 3: 0}[g]
                        act.wait_ge(st_full, since(b, st_full, ST[("fst", user, T - 1, GH - 1)], g == 2))
                        dst = (fq if kind == "fq" else fk)[:, g % 3]
                    elif kind in ("tq", "tk"):
                        h = x_[1]
                        act.wait_ge(st_full, since(b, st_full, ST[("st", (h - 4) % H, 2)], h < 4))
                        dst = (q_hm if kind == "tq" else k_hh)[:, h % 4]
                    elif kind == "cT":
                        act.wait_ge(wk_full, past(b, wk_full, FULL[("moe", T - 1, 1)]))
                        dst = ct_h[:]
                    else:
                        act.wait_ge(wk_full, now(b, wk_full, FULL[("wo",)]))
                        dst = ct_h[:]
                    nc.scalar.copy(dst, src).then_inc(open_rounded if x_ in OPEN_SPLIT else rounded, 1)
                elif x_ in V_ACT:
                    _, t, half = x_
                    act.wait_ge(wk_full, now(b, wk_full, FULL[x_]))
                    if t == 0:
                        act.wait_ge(o_full, past(b, o_full, PG))
                    nc.scalar.copy(v[:, t, 0:H // 2], wk_of(x_)[:].rearrange("p (h d) -> p h d", d=DH)).then_inc(v_act, 1)
                elif kind == "mT":
                    act.wait_ge(wk_full, now(b, wk_full, FULL[x_]))
                    nc.scalar.copy(q_hm[64:65, x_[1] % 4], wk_of(x_)[64:65, :]).then_inc(row_done, 1)
                elif kind == "st":
                    _, h, unit = x_
                    act.wait_ge(st_full, now(b, st_full, ST[x_]))
                    if unit == 0:
                        act.wait_ge(o_full, since(b, o_full, (h - 3) % H // 2 + 1 if h >= 3 else PG, h < 3))
                    nc.scalar.activation(pt[:, h % 3, PT_AT[unit]:PT_AT[unit] + ST_N[unit]],
                                         st_bank[(ST[x_] - 1) % 2][:, 0:ST_N[unit]],
                                         ACT.Exp, scale=1.0 / math.sqrt(DH)).then_inc(exp_done, 1)
                elif kind == "fst":
                    _, g, i, f = x_
                    act.wait_ge(st_full, now(b, st_full, ST[x_]))
                    if f == 0:
                        m = g * T + i - 2
                        act.wait_ge(f_summed, since(b, f_summed, m % (G * T) + 1, m < 0))
                    nc.scalar.activation(fpt[:, i % 2, f], st_bank[(ST[x_] - 1) % 2][:],
                                         ACT.Exp, scale=1.0 / math.sqrt(FD)).then_inc(exp_done, 1)
                elif kind == "fpv" and x_[2] == T - 1:
                    g = x_[1]
                    act.wait_ge(f_summed, now(b, f_summed, g * T + T))
                    if g:
                        act.wait_ge(wk_full, now(b, wk_full, FULL[("fT", g - 1)]))
                    else:
                        act.wait_ge(wk_full, past(b, wk_full, FULL[("fT", G - 1)]))
                    nc.scalar.copy(fo[:], f_bank[:]).then_inc(fo_done, 1)
                elif kind == "pv" and x_[2] == T - 1:
                    c = x_[1]
                    act.wait_ge(divided, now(b, divided, c + 1))
                    act.wait_ge(wk_full, since(b, wk_full, FULL[("attn", (c - 2) % PG)], c < 2))
                    nc.scalar.copy(u_h[:, c % 2], u[:]).then_inc(u_rounded, 1)
                elif kind == "gate":
                    act.wait_ge(logits, now(b, logits, 1))
                    nc.scalar.activation(gexp, glog, ACT.Exp).then_inc(gate_exp, 1)

            for x_ in OPENING:
                step(-1, x_)
            with act.Fori(0, B) as b:
                for x_ in PLAN:
                    step(b, x_)

        @block.vector
        def _(dve):
            nc.vector.memset(raw_bias, 0.0).then_inc(prepared, 1)
            nc.vector.memset(fnmax[:], 0.0)
            nc.vector.memset(k_l1[:].bitcast(F32), 1.0)
            nc.vector.memset(ones[:], 1.0)
            nc.vector.memset(f_bank[:], 0.0)
            nc.vector.memset(fv[:].rearrange("p t h d -> p (t h) d")[:, :, FD:FVW], 1.0)
            nc.vector.memset(strips_h[:].bitcast(F32), 0.0)
            nc.vector.memset(strips_l[:].bitcast(F32), 0.0).then_inc(prep_dve, 1)
            dve.wait_ge(loaded, 16 * N_LOADS)
            row_k, at_k, n_k = BIAS["bk"]
            nc.vector.memset(raw_bias[row_k:row_k + 1, at_k:at_k + n_k].rearrange("p (h c) -> p h c", c=STRIP)[:, :, 0:1],
                             1.0).then_inc(prep_dve, 1)
            nc.vector.tensor_copy(masks[:, 0], ident)
            nc.vector.tensor_copy(masks[:, 1:3], raw_masks)
            dve.wait_ge(prep_dve, 2)
            nc.vector.tensor_copy(hi_bias, raw_bias).then_inc(prep_dve, 1)
            dve.wait_ge(prep_dve, 3)
            nc.vector.scalar_tensor_tensor(out=biases[:], in0=hi_bias.bitcast(F32), scalar=second, in1=raw_bias,
                                           op0=ALU.mult, op1=ALU.add).then_inc(prep_dve, 1)
            dve.wait_ge(prep_dve, 4)
            nc.vector.memset(biases[:, ONES:BIAS_N].bitcast(F32), 1.0)
            nc.vector.memset(biases[BIAS["bq"][0]:BIAS["bq"][0] + 2, S:2 * S].bitcast(F32), 1.0)
            nc.vector.memset(biases[BIAS["bk"][0]:BIAS["bk"][0] + 2, S:2 * S].bitcast(F32), 1.0)
            for n in range(2):
                src = raw_qk[:, n * D:(n + 1) * D].rearrange("p (h d) -> p h d", d=FD)
                for c in range(1, 4):
                    nc.vector.tensor_copy(strips_h[:, n, :, c * FD:(c + 1) * FD], src).then_inc(prep_dve, 1)
            dve.wait_ge(prep_dve, 10)
            for n in range(2):
                src = raw_qk[:, n * D:(n + 1) * D].rearrange("p (h d) -> p h d", d=FD)
                for c in range(1, 4):
                    nc.vector.tensor_tensor(strips_l[:, n, :, c * FD:(c + 1) * FD], src,
                                            strips_h[:, n, :, c * FD:(c + 1) * FD].bitcast(F32), ALU.subtract)
            dve.wait_ge(prepared, 5)
            nc.vector.tensor_tensor(wqkv_l[:], raw_qkv, wqkv_h[:].bitcast(F32), ALU.subtract)
            nc.vector.tensor_tensor(wout_l[:], raw_out, wout_h[:].bitcast(F32), ALU.subtract)
            nc.vector.tensor_tensor(we_l[:], raw_we, we_h[:].bitcast(F32), ALU.subtract)
            nc.vector.tensor_tensor(small_l[:], raw_small, small_h[:].bitcast(F32), ALU.subtract).then_inc(prep_dve, 1)
            dve.wait_ge(prep_dve, 11)
            dve.drain().then_inc(prepared, 1)
            start(dve, split, v_dve, turned, variance, max_done, fmax_done, divided, fdivided, misc_read, x2_done, logits,
                  step_done)

            def carry_wait():
                nc.vector.memset(spare[:], 0.0)

            taken = [0]

            def next_step():
                taken[0] += 1
                return taken[0]

            def layernorm(b, n, src):
                for t in range(T - 1):
                    nc.vector.bn_stats(stats[:, t], src(t))
                nc.vector.bn_stats(stats[:, T - 1], src(T - 1)).then_inc(step_done, 1)
                dve.wait_ge(step_done, now(b, step_done, next_step()))
                carry_wait()
                for t in range(T - 1):
                    nc.vector.bn_aggr(moments[:, t], stats[:, t])
                nc.vector.bn_aggr(moments[:, T - 1], stats[:, T - 1]).then_inc(step_done, 1)
                dve.wait_ge(step_done, now(b, step_done, next_step()))
                nc.vector.tensor_scalar(spread[:].unsqueeze(2), moments[:, :, 1:2], EPS, None, ALU.add).then_inc(variance, 1)
                dve.wait_ge(rstd_done, now(b, rstd_done, n))

            def step(b, x_):
                kind = x_[0]
                if x_ in WK_AT and kind not in SPLIT_KINDS:
                    full, n_full = full_of(x_)
                    dve.wait_ge(full, now(b, full, n_full))
                if kind == "ln":
                    dve.wait_ge(x_loaded, b * 16 + 32)
                    for t in range(T - 1):
                        nc.vector.bn_stats(stats[:, t], x_in[:, t])
                    nc.vector.bn_stats(stats[:, T - 1], x_in[:, T - 1]).then_inc(open_step, 1)
                    dve.wait_ge(open_step, now(b, open_step, 1))
                    carry_wait()
                    for t in range(T - 1):
                        nc.vector.bn_aggr(moments[:, t], stats[:, t])
                    nc.vector.bn_aggr(moments[:, T - 1], stats[:, T - 1]).then_inc(open_step, 1)
                    dve.wait_ge(open_step, now(b, open_step, 2))
                    nc.vector.tensor_scalar(spread_x[:].unsqueeze(2), moments[:, :, 1:2], EPS, None, ALU.add)\
                        .then_inc(x_variance, 1)
                    dve.wait_ge(x_rstd, now(b, x_rstd, 1))
                    dve.wait_ge(wk_full, now(b, wk_full, FULL[("x2T",)]))
                    for t in range(T - 1):
                        nc.vector.tensor_scalar(xn[:, t], x_in[:, t], moments[:, t, 0:1], rstd_x[:, t:t + 1],
                                                ALU.subtract, ALU.mult)
                    nc.vector.tensor_scalar(xn[:, T - 1], x_in[:, T - 1], moments[:, T - 1, 0:1], rstd_x[:, T - 1:T],
                                            ALU.subtract, ALU.mult).then_inc(normal, 1)
                elif kind in SPLIT_KINDS:
                    opening = x_ in OPEN_SPLIT
                    if opening:
                        dve.wait_ge(open_rounded, now(b, open_rounded, OPEN_SPLIT[x_]))
                    else:
                        dve.wait_ge(rounded, now(b, rounded, SPLIT[x_]))
                    src = wk_of(x_)[:]
                    if kind == "xT":
                        ins = nc.vector.tensor_tensor(xt_l[:], src, xt_h[:].bitcast(F32), ALU.subtract)
                    elif kind in ("fq", "fk"):
                        strips = (fq if kind == "fq" else fk)[:, x_[1] % 3]
                        ins = nc.vector.scalar_tensor_tensor(
                            out=strips, in0=strips.bitcast(F32), scalar=q_low if kind == "fq" else k_low, in1=src,
                            op0=ALU.mult, op1=ALU.add)
                    elif kind == "tq":
                        h = x_[1]
                        ins = nc.vector.scalar_tensor_tensor(out=q_hl[:, h % 4], in0=q_hm[:, h % 4].bitcast(F32),
                                                             scalar=low_rows, in1=src, op0=ALU.mult, op1=ALU.add)
                    elif kind == "tk":
                        h = x_[1]
                        ins = nc.vector.tensor_tensor(k_l1[0:DH, h % 4], src[0:DH], k_hh[0:DH, h % 4].bitcast(F32),
                                                      ALU.subtract)
                    else:
                        ins = nc.vector.tensor_tensor(ct_l[:], src, ct_h[:].bitcast(F32), ALU.subtract)
                    ins.then_inc(open_split if opening else split, 1)
                elif kind == "v" and x_ in V_DVE:
                    _, t, half = x_
                    if t == 0:
                        dve.wait_ge(o_full, past(b, o_full, PG))
                    nc.vector.tensor_copy(v[:, t, H // 2:H], wk_of(x_)[:].rearrange("p (h d) -> p h d", d=DH)).then_inc(v_dve, 1)
                elif kind == "fv":
                    dve.wait_ge(f_summed, past(b, f_summed, G * T))
                    nc.vector.tensor_copy(fv[:, :, :, 0:FD],
                                          wk_of(x_)[:].rearrange("p (t h d) -> p t h d", t=T, d=FD)).then_inc(v_dve, 1)
                elif kind == "proj":
                    _, g, pair = x_
                    for k in range(2):
                        t, n = 2 * pair + k, 2 * PROJ[x_] - 1 + k
                        dve.wait_ge(rotated, since(b, rotated, (n - 3) % (2 * len(PROJ)) + 1, n < 3))
                        w = 2 * PH * DH
                        src = wk_of(x_)[:, k * w:(k + 1) * w]
                        cos = angles[:, t, 0:DH // 2].unsqueeze(1).unsqueeze(3).broadcast_to([P, 2 * PH, DH // 2, 2])
                        sin = angles[:, t, DH // 2:].unsqueeze(1).broadcast_to([P, 2 * PH, DH])
                        nc.vector.tensor_tensor(rot[:, n % 2, 0].rearrange("p (h i two) -> p h i two", two=2, i=DH // 2),
                                                src.rearrange("p (h i two) -> p h i two", two=2, i=DH // 2), cos, ALU.mult)
                        nc.vector.tensor_tensor(rot[:, n % 2, 1].rearrange("p (h d) -> p h d", d=DH),
                                                src.rearrange("p (h d) -> p h d", d=DH), sin, ALU.mult).then_inc(turned, 1)
                elif kind == "sm":
                    _, h, unit = x_
                    if unit == 0:
                        dve.wait_ge(wk_full, since(b, wk_full, FULL[("mT", (h - 4) % H)], h < 4))
                    units = SM_UNITS[unit]
                    for j, at in units[:-1]:
                        nc.vector.tensor_reduce(nmax[:, h % 4, j:j + 1], wk_of(x_)[:, at:at + (j + 1) * P],
                                                AX.X, ALU.max, negate=True)
                    j, at = units[-1]
                    nc.vector.tensor_reduce(nmax[:, h % 4, j:j + 1], wk_of(x_)[:, at:at + (j + 1) * P],
                                            AX.X, ALU.max, negate=True).then_inc(max_done, 1)
                elif kind == "fsm":
                    _, f, j = x_
                    if f % GH == 0 and j == 0:
                        g = f // GH
                        dve.wait_ge(wk_full, now(b, wk_full, FULL[("fmT", (g - 1) % G)]))
                    nc.vector.tensor_reduce(fnmax[:, j, f % GH, 0:1], wk_of(x_)[:], AX.X, ALU.max, negate=True)\
                        .then_inc(max_done, 1)
                elif kind == "fmT":
                    g = x_[1]
                    nc.vector.tensor_tensor(fq[:, g % 3], wk_of(x_)[:], fq[:, g % 3].bitcast(F32), ALU.add).then_inc(fmax_done, 1)
                elif kind == "pv" and x_[2] == T - 1:
                    c = x_[1]
                    dve.wait_ge(o_full, now(b, o_full, c + 1))
                    dve.wait_ge(u_split, since(b, u_split, (c - 1) % PG + 1, c == 0))
                    nc.vector.reciprocal(u[:], l_bank[:]).then_inc(step_done, 1)
                    dve.wait_ge(step_done, now(b, step_done, next_step()))
                    nc.vector.tensor_tensor(u[:], o_bank[:], u[:], ALU.mult).then_inc(divided, 1)
                elif kind == "fT":
                    g = x_[1]
                    bank = wk_of(x_)[:].rearrange("p (t f c) -> p t f c", f=GH, c=STRIP)
                    nc.vector.reciprocal(frec[:].unsqueeze(3), bank[:, :, :, FD:FVW]).then_inc(step_done, 1)
                    dve.wait_ge(step_done, now(b, step_done, next_step()))
                    if g == 0:
                        dve.wait_ge(wk_full, past(b, wk_full, FULL[("cT",)]))
                    nc.vector.tensor_tensor(
                        ct[:, :, g * GH * FD:(g + 1) * GH * FD].rearrange("p t (f d) -> p t f d", d=FD),
                        bank[:, :, :, 0:FD], frec[:].unsqueeze(3).broadcast_to([P, T, GH, FD]), ALU.mult).then_inc(fdivided, 1)
                elif kind == "attn":
                    src = wk_of(x_)[:].rearrange("p (t d) -> p t d", d=D)
                    if x_[1] == 0:
                        dve.wait_ge(out_sent, b * 16 + 16)
                        nc.vector.tensor_tensor(y[:], src, x_in[:], ALU.add).then_inc(misc_read, 1)
                    else:
                        dve.wait_ge(misc_read, now(b, misc_read, MISC[x_] - 1))
                        nc.vector.tensor_tensor(y[:], src, y[:], ALU.add).then_inc(misc_read, 1)
                elif kind == "wo":
                    src = wk_of(x_)[:].rearrange("p (t d) -> p t d", d=D)
                    layernorm(b, 1, lambda t: src[:, t])
                    for t in range(T - 1):
                        nc.vector.tensor_scalar(branch[:, t], src[:, t], moments[:, t, 0:1], rstd[:, t:t + 1],
                                                ALU.subtract, ALU.mult)
                    nc.vector.tensor_scalar(branch[:, T - 1], src[:, T - 1], moments[:, T - 1, 0:1], rstd[:, T - 1:T],
                                            ALU.subtract, ALU.mult).then_inc(misc_read, 1)
                    dve.wait_ge(misc_read, now(b, misc_read, MISC[x_]))
                    nc.vector.tensor_tensor(branch[:], branch[:], affine[:, 0].unsqueeze(1).broadcast_to([P, T, D]),
                                            ALU.mult).then_inc(step_done, 1)
                    dve.wait_ge(step_done, now(b, step_done, next_step()))
                    nc.vector.tensor_tensor(branch[:], branch[:], affine[:, 1].unsqueeze(1).broadcast_to([P, T, D]),
                                            ALU.add).then_inc(step_done, 1)
                    dve.wait_ge(step_done, now(b, step_done, next_step()))
                    nc.vector.tensor_tensor(x2[:], branch[:], xn[:], ALU.add).then_inc(x2_done, 1)
                    dve.wait_ge(x2_done, now(b, x2_done, 1))
                    nc.vector.tensor_tensor(y[:], y[:], x2[:], ALU.add).then_inc(step_done, 1)
                    dve.wait_ge(step_done, now(b, step_done, next_step()))
                elif kind == "gate":
                    src = wk_of(x_)[:, 0:T * E].rearrange("p (t e) -> p t e", e=E)
                    wide = [P, T, E]
                    nc.vector.tensor_reduce(gmax[:].unsqueeze(2), src, AX.X, ALU.max, negate=True).then_inc(step_done, 1)
                    dve.wait_ge(step_done, now(b, step_done, next_step()))
                    nc.vector.tensor_tensor(glog, src, gmax[:].unsqueeze(2).broadcast_to(wide), ALU.add).then_inc(step_done, 1)
                    dve.wait_ge(step_done, now(b, step_done, next_step()))
                    nc.vector.memset(gtop[:], 0.0).then_inc(misc_read, 1)
                    nc.vector.memset(gidx, 0).then_inc(logits, 1)
                elif kind == "pick":
                    wide = [P, T, E]
                    dve.wait_ge(gate_exp, now(b, gate_exp, 1))
                    nc.vector.tensor_reduce(gsum[:].unsqueeze(2), gexp, AX.X, ALU.add).then_inc(step_done, 1)
                    dve.wait_ge(step_done, now(b, step_done, next_step()))
                    nc.vector.reciprocal(grec[:], gsum[:]).then_inc(step_done, 1)
                    dve.wait_ge(step_done, now(b, step_done, next_step()))
                    nc.vector.tensor_tensor(gprob, gexp, grec[:].unsqueeze(2).broadcast_to(wide), ALU.mult)\
                        .then_inc(step_done, 1)
                    dve.wait_ge(step_done, now(b, step_done, next_step()))
                    carry_wait()
                    for t in range(T - 1):
                        nc.vector.max(gtop[:, t], gprob[:, t])
                    nc.vector.max(gtop[:, T - 1], gprob[:, T - 1]).then_inc(step_done, 1)
                    dve.wait_ge(step_done, now(b, step_done, next_step()))
                    carry_wait()
                    for t in range(T - 1):
                        nc.vector.max_index(gidx[:, t], gtop[:, t], gprob[:, t])
                    nc.vector.max_index(gidx[:, T - 1], gtop[:, T - 1], gprob[:, T - 1]).then_inc(step_done, 1)
                    dve.wait_ge(step_done, now(b, step_done, next_step()))
                    nc.vector.tensor_copy(gidf, gidx).then_inc(step_done, 1)
                    dve.wait_ge(step_done, now(b, step_done, next_step()))
                    iota = experts.unsqueeze(1).broadcast_to(wide)
                    nc.vector.tensor_tensor(gate_a, iota, gidf[:, :, 0:1].broadcast_to(wide), ALU.is_equal)
                    nc.vector.tensor_tensor(gate_b, iota, gidf[:, :, 1:2].broadcast_to(wide), ALU.is_equal)\
                        .then_inc(step_done, 1)
                    dve.wait_ge(step_done, now(b, step_done, next_step()))
                    nc.vector.tensor_tensor(gate_a, gate_a, gtop[:, :, 0:1].broadcast_to(wide), ALU.mult)
                    nc.vector.tensor_tensor(gate_b, gate_b, gtop[:, :, 1:2].broadcast_to(wide), ALU.mult)\
                        .then_inc(step_done, 1)
                    dve.wait_ge(step_done, now(b, step_done, next_step()))
                    nc.vector.tensor_tensor(gate_w[:], gate_a, gate_b, ALU.add).then_inc(step_done, 1)
                    dve.wait_ge(step_done, now(b, step_done, next_step()))
                elif kind == "moe":
                    _, t, half = x_
                    e0 = half * HALF
                    nc.vector.tensor_tensor(
                        weighted[:, e0:e0 + HALF], wk_of(x_)[:].rearrange("p (e d) -> p e d", d=D),
                        gate_w[:, t, e0:e0 + HALF].unsqueeze(2).broadcast_to([P, HALF, D]), ALU.mult).then_inc(misc_read, 1)
                    if half == 1:
                        dve.wait_ge(misc_read, now(b, misc_read, MISC[x_]))
                        nc.vector.tensor_reduce(branch[:, t].unsqueeze(2), weighted[:].rearrange("p e d -> p d e"),
                                                AX.X, ALU.add).then_inc(step_done, 1)
                        dve.wait_ge(step_done, now(b, step_done, next_step()))
                elif kind == "norm":
                    layernorm(b, 2, lambda t: branch[:, t])
                    for t in range(T - 1):
                        nc.vector.tensor_scalar(branch[:, t], branch[:, t], moments[:, t, 0:1], rstd[:, t:t + 1],
                                                ALU.subtract, ALU.mult)
                    nc.vector.tensor_scalar(branch[:, T - 1], branch[:, T - 1], moments[:, T - 1, 0:1], rstd[:, T - 1:T],
                                            ALU.subtract, ALU.mult).then_inc(step_done, 1)
                    dve.wait_ge(step_done, now(b, step_done, next_step()))
                    nc.vector.tensor_tensor(branch[:], branch[:], affine[:, 2].unsqueeze(1).broadcast_to([P, T, D]),
                                            ALU.mult).then_inc(step_done, 1)
                    dve.wait_ge(step_done, now(b, step_done, next_step()))
                    nc.vector.tensor_tensor(branch[:], branch[:], affine[:, 3].unsqueeze(1).broadcast_to([P, T, D]),
                                            ALU.add).then_inc(step_done, 1)
                    dve.wait_ge(step_done, now(b, step_done, next_step()))
                    dve.wait_ge(misc_read, now(b, misc_read, MISC[("attn", PG - 2)]))
                    nc.vector.tensor_tensor(y[:], branch[:], y[:], ALU.add).then_inc(step_done, 1)
                    dve.wait_ge(step_done, now(b, step_done, next_step()))

            for x_ in OPENING:
                step(-1, x_)
            with dve.Fori(0, B) as b:
                taken[0] = 0
                for x_ in PLAN:
                    step(b, x_)
                assert taken[0] == N_STEP, taken

        @block.tensor
        def _(pe):
            start(pe, wk_full, st_full, o_full, f_summed)
            pe.sem_inc(out_sent, 16)
            pe.wait_ge(prepared, 6)

            def split3(dst, lh, ll, rh, rl, bias=None):
                nc.tensor.matmul(dst, lh, rh, start=True, stop=False)
                nc.tensor.matmul(dst, ll, rh, start=False, stop=False)
                ins = nc.tensor.matmul(dst, lh, rl, start=False, stop=bias is None)
                if bias is not None:
                    ins = nc.tensor.matmul(dst, bias[0], bias[1], start=False, stop=True)
                return ins

            def bias_rows(name, a=0, n=None):
                p0, at, whole = BIAS[name]
                return biases[p0:p0 + 2, at + a:at + a + (n or whole)]

            def one_rows(name):
                return biases[BIAS[name][0]:BIAS[name][0] + 2, ONES:ONES + P]

            def transposed(bank, src):
                for t in range(T):
                    n = src(t).shape[-1]
                    ins = nc.tensor.transpose(bank[0:n, t * P:(t + 1) * P], src(t), ident)
                return ins

            def step(b, x_):
                kind = x_[0]
                full = open_full if x_ in OPEN_FULL else wk_full
                if x_ in WK_AT:
                    n = WK_AT[x_]
                    read, c = bank_read(WK_LIST[n - WK_BANKS])
                    if n >= WK_BANKS:
                        pe.wait_ge(read, now(b, read, c))
                    else:
                        pe.wait_ge(read, past(b, read, c))
                    bank = wk_of(x_)
                if kind in ("fq", "fk", "proj", "v", "fv"):
                    pe.wait_ge(open_split, since(b, open_split, OPEN_SPLIT[("xT",)], x_ not in OPENING))
                if kind == "xT":
                    pe.wait_ge(normal, now(b, normal, 1))
                    transposed(bank, lambda t: xn[:, t]).then_inc(full, 1)
                elif kind == "v":
                    _, t, half = x_
                    a = 2 * H * DH + half * 512
                    tok = slice(t * P, (t + 1) * P)
                    split3(bank[:], xt_h[:, tok], xt_l[:, tok], wqkv_h[:, a:a + 512], wqkv_l[:, a:a + 512]).then_inc(full, 1)
                elif kind == "fv":
                    for t in range(T):
                        tok = slice(t * P, (t + 1) * P)
                        ins = split3(bank[:, tok], xt_h[:, tok], xt_l[:, tok], small_h[:, 0:D], small_l[:, 0:D],
                                     (one_rows("bv"), bias_rows("bv")))
                    ins.then_inc(full, 1)
                elif kind in ("fq", "fk"):
                    g, n = x_[1], int(kind == "fk")
                    wh = strips_h[:, n, g * GH:(g + 1) * GH].rearrange("p h c -> p (h c)")
                    wl = strips_l[:, n, g * GH:(g + 1) * GH].rearrange("p h c -> p (h c)")
                    name = "bk" if n else "bq"
                    split3(bank[:], wh, wl, xt_h[:], xt_l[:], (bias_rows(name, g * P, P),
                           biases[BIAS[name][0]:BIAS[name][0] + 2, S:2 * S])).then_inc(full, 1)
                elif kind == "proj":
                    _, g, pair = x_
                    n = PH * DH
                    w = [a[:].rearrange("p (k n) -> p k n", n=H * DH)[:, 0:2, g * n:(g + 1) * n] for a in (wqkv_h, wqkv_l)]
                    for t in range(2 * pair, 2 * pair + 2):
                        tok, at = slice(t * P, (t + 1) * P), t % 2 * 2 * n
                        ins = split3(bank[:, at:at + 2 * n], xt_h[:, tok], xt_l[:, tok], w[0], w[1])
                    ins.then_inc(full, 1)
                elif kind in ("tq", "tk"):
                    h = x_[1]
                    g, k = h // PH, int(kind == "tk")
                    if h % PH == 0:
                        pe.wait_ge(rotated, since(b, rotated, 2 * PROJ[("proj", g, 1)], g == 0))
                    transposed(bank, lambda t: qk[:, g % 2, t, k * PH + h % PH].rearrange("p r d -> p (r d)")).then_inc(full, 1)
                elif kind == "mT":
                    h = x_[1]
                    pe.wait_ge(max_done, now(b, max_done, MAX[("sm", h, 2)]))
                    transposed(bank, lambda t: nmax[:, h % 4, t:t + 1].broadcast_to([P, DH + 1])).then_inc(full, 1)
                elif kind == "fmT":
                    g = x_[1]
                    pe.wait_ge(max_done, since(b, max_done, MAX[("fsm", GH * g + GH - 1, T - 1)], g == 0))
                    transposed(bank, lambda t: fnmax[:, t].rearrange("p h c -> p (h c)")).then_inc(full, 1)
                elif kind == "sm":
                    _, h, unit = x_
                    if unit == 0:
                        pe.wait_ge(split, now(b, split, SPLIT[("tk", h)]))
                    for j, at in SM_UNITS[unit]:
                        nc.tensor.matmul(bank[:, at:at + (j + 1) * P], q_hl[:, h % 4, j * P:(j + 1) * P],
                                         k_hh[:, h % 4, 0:(j + 1) * P], start=True, stop=True)
                        ins = nc.tensor.matmul(bank[:, at + j * P:at + (j + 1) * P], masks[:, 0], masks[:, 1],
                                               start=False, stop=True, skip_group_check=True)
                    ins.then_inc(full, 1)
                elif kind == "fsm":
                    _, f, j = x_
                    g, r = f // GH, slice(f % GH * STRIP, (f % GH + 1) * STRIP)
                    if f % GH == 0 and j == 0:
                        if g < 2:
                            pe.wait_ge(open_split, since(b, open_split, OPEN_SPLIT[("fk", g)], g == 1))
                        else:
                            pe.wait_ge(split, now(b, split, SPLIT[("fk", g)]))
                    nc.tensor.matmul(bank[:], fq[r, g % 3, j * P:(j + 1) * P], fk[r, g % 3], start=True, stop=True,
                                     tile_position=(r.start, 0)).then_inc(full, 1)
                elif kind == "st":
                    _, h, unit = x_
                    if unit == 0:
                        pe.wait_ge(row_done, now(b, row_done, h + 1))
                    n = ST[x_]
                    pe.wait_ge(exp_done, since(b, exp_done, (n - 3) % len(ST) + 1, n < 3))
                    for i, at in ST_UNITS[unit]:
                        dst = st_bank[(n - 1) % 2][:, at:at + S - i * P]
                        nc.tensor.matmul(dst, k_hh[:, h % 4, i * P:(i + 1) * P], q_hl[:, h % 4, i * P:S],
                                         start=True, stop=False)
                        nc.tensor.matmul(dst, k_l1[0:DH + 1, h % 4, i * P:(i + 1) * P], q_hm[0:DH + 1, h % 4, i * P:S],
                                         start=False, stop=True)
                        ins = nc.tensor.matmul(dst[:, 0:P], masks[:, 0], masks[:, 2],
                                               start=False, stop=True, skip_group_check=True)
                    ins.then_inc(st_full, 1)
                elif kind == "fst":
                    _, g, i, f = x_
                    r = slice(f * STRIP, (f + 1) * STRIP)
                    if i == 0 and f == 0:
                        pe.wait_ge(fmax_done, now(b, fmax_done, g + 1))
                    n = ST[x_]
                    pe.wait_ge(exp_done, since(b, exp_done, (n - 3) % len(ST) + 1, n < 3))
                    nc.tensor.matmul(st_bank[(n - 1) % 2][:], fk[r, g % 3, i * P:(i + 1) * P], fq[r, g % 3],
                                     start=True, stop=True, tile_position=(r.start, 0)).then_inc(st_full, 1)
                elif kind == "pv":
                    _, c, i = x_
                    if i == 0:
                        pe.wait_ge(exp_done, now(b, exp_done, ST[("st", 2 * c + 1, 2)]))
                        pe.wait_ge(divided, since(b, divided, (c - 1) % PG + 1, c == 0))
                        if c == 0:
                            pe.wait_ge(v_act, now(b, v_act, len(V_ACT)))
                            pe.wait_ge(v_dve, now(b, v_dve, len(V_DVE)))
                    for bank, sums in ((o_bank, False), (l_bank, True)):
                        for r in range(2):
                            h = 2 * c + r
                            ins = nc.tensor.matmul(bank[r * DH:(r + 1) * DH, i * P:S], ones[:] if sums else v[:, i, h],
                                                   pt[:, h % 3, PT_AT[i]:PT_AT[i] + S - i * P],
                                                   start=(i == 0), stop=(i == T - 1), tile_position=(0, r * DH))
                    if i == T - 1:
                        ins.then_inc(o_full, 1)
                elif kind == "fpv":
                    _, g, i = x_
                    pe.wait_ge(exp_done, now(b, exp_done, ST[("fst", g, i, GH - 1)]))
                    if i == 0:
                        pe.wait_ge(fo_done, since(b, fo_done, (g - 1) % G + 1, g == 0))
                        if g == 0:
                            pe.wait_ge(v_dve, now(b, v_dve, V_DVE[("fv",)]))
                    for f in range(GH):
                        ins = nc.tensor.matmul(f_bank[f * STRIP:f * STRIP + FVW], fv[:, i, g * GH + f], fpt[:, i % 2, f],
                                               start=(i == 0), stop=(i == T - 1), tile_position=(0, f * STRIP))
                    ins.then_inc(f_summed, 1)
                elif kind == "fT":
                    g = x_[1]
                    pe.wait_ge(fo_done, now(b, fo_done, g + 1))
                    transposed(bank, lambda t: fo[:, t * P:(t + 1) * P]).then_inc(full, 1)
                elif kind == "attn":
                    c = x_[1]
                    pe.wait_ge(u_rounded, now(b, u_rounded, c + 1))
                    pe.wait_ge(u_split, now(b, u_split, c + 1))
                    for t in range(T):
                        tok = slice(t * P, (t + 1) * P)
                        ins = split3(bank[:, tok], u_h[:, c % 2, tok], u_l[:, c % 2, tok], wout_h[:, c], wout_l[:, c])
                    ins.then_inc(full, 1)
                elif kind == "cT":
                    pe.wait_ge(fdivided, now(b, fdivided, G))
                    transposed(bank, lambda t: ct[:, t]).then_inc(full, 1)
                elif kind == "wo":
                    pe.wait_ge(split, now(b, split, SPLIT[("cT",)]))
                    for t in range(T):
                        tok = slice(t * P, (t + 1) * P)
                        ins = split3(bank[:, tok], ct_h[:, tok], ct_l[:, tok], small_h[:, D:2 * D], small_l[:, D:2 * D],
                                     (one_rows("bo"), bias_rows("bo")))
                    ins.then_inc(full, 1)
                elif kind == "x2T":
                    pe.wait_ge(x2_done, now(b, x2_done, 1))
                    transposed(bank, lambda t: x2[:, t]).then_inc(full, 1)
                elif kind == "gate":
                    pe.wait_ge(split, now(b, split, SPLIT[("x2T",)]))
                    for t in range(T):
                        tok = slice(t * P, (t + 1) * P)
                        ins = split3(bank[:, t * E:(t + 1) * E], x2t_h[:, tok], x2t_l[:, tok],
                                     small_h[:, 2 * D:2 * D + E], small_l[:, 2 * D:2 * D + E],
                                     (one_rows("bg"), bias_rows("bg")))
                    ins.then_inc(full, 1)
                elif kind == "moe":
                    _, t, half = x_
                    tok = slice(t * P, (t + 1) * P)
                    e = slice(half * HALF, (half + 1) * HALF)
                    split3(bank[:], x2t_h[:, tok], x2t_l[:, tok], we_h[:, e].rearrange("p e d -> p (e d)"),
                           we_l[:, e].rearrange("p e d -> p (e d)"),
                           (one_rows("bexp"), bias_rows("bexp", half * 512, 512))).then_inc(full, 1)

            for x_ in OPENING:
                step(-1, x_)
            with pe.Fori(0, B) as b:
                for x_ in PLAN:
                    step(b, x_)


_INS = ["L0_attn_x", "L0_attn_W_qkv", "L0_attn_W_out", "L0_ffn_Wq", "L0_ffn_bq", "L0_ffn_Wk", "L0_ffn_bk", "L0_ffn_Wv",
        "L0_ffn_bv", "L0_ffn_Wo", "L0_ffn_bo", "L0_ffn_g1", "L0_ffn_be1", "L0_ffn_g2", "L0_ffn_be2", "L0_ffn_Wg",
        "L0_ffn_bg", "L0_ffn_We", "L0_ffn_bexp"]


def _tables():
    import numpy as np

    table = np.zeros((P, C_MT + P), np.float32)
    p, n = np.arange(P)[:, None], np.arange(P)[None, :]
    table[:, C_ID:C_ID + P] = p == n
    table[:, C_MS:C_MS + P] = np.where(n > p, -1e30, 0)
    table[:, C_MT:C_MT + P] = np.where(p > n, -1e30, 0)
    row = np.arange(P) % STRIP
    table[:, C_COL] = np.where(np.arange(P) >= DH, -1, 0)
    table[:, C_COL + 1] = np.where((row >= 2 * FD) & (row < 3 * FD), -1, 0)
    table[:, C_COL + 2] = np.where(row >= 3 * FD, -1, 0)
    table[:, C_COL + 3] = np.where(row == 1, -1, 0)
    table[:, C_IOTA:C_IOTA + E] = np.arange(E)
    pairs = np.arange(0, DH, 2).astype(np.float32)
    freqs = (np.float32(1.0) / np.float32(10000.0) ** (pairs / np.float32(DH))).astype(np.float32)
    angle = (np.arange(S).astype(np.float32)[:, None] * freqs[None, :]).astype(np.float32)
    sines = np.stack([np.sin(angle), -np.sin(angle)], 2).reshape(S, DH)
    rope = np.concatenate([np.cos(angle), sines], 1).astype(np.float32)
    return table, rope


def kernel(**inputs):
    import numpy as _np
    import concourse.bacc as _bacc
    from concourse import mybir as _mybir
    from concourse.bass_utils import run_bass_kernel_spmd as _run

    nc = _bacc.Bacc("TRN2", target_bir_lowering=False, num_devices=1)
    table, rope = _tables()
    given = {name: _np.ascontiguousarray(inputs[name]) for name in _INS}
    given["table"], given["rope"] = table, rope
    arrays, args = {}, []
    for name, a in given.items():
        arrays[f"in_{name}_dram"] = a
        args.append(nc.dram_tensor(f"in_{name}_dram", a.shape, _mybir.dt.from_np(a.dtype), kind="ExternalInput").ap())
    args.append(nc.dram_tensor("out_0_dram", (B, S, D), _mybir.dt.float32, kind="ExternalOutput").ap())
    build(nc, *args)
    r = _run(nc, [arrays], core_ids=[0])
    return r.results[0]["out_0_dram"]
```

```python
import concourse.bass as bass
from concourse import mybir
from contextlib import ExitStack
import math

F32 = mybir.dt.float32
F32R = mybir.dt.float32r
BF16 = mybir.dt.bfloat16
U32 = mybir.dt.uint32
ALU = mybir.AluOpType
ACT = mybir.ActivationFunctionType
AX = mybir.AxisListType

B, S, D = 8, 512, 128
P = 128
T = S // P
H, DH = 16, 64
FH, FD = 16, 8
PH = 2
PG = H // PH
GH = 4
G = FH // GH
E = 8
STRIP = 32
EPS = 1e-5
FVW = FD + 1
HALF = 512 // D

BIAS = {"bexp": (0, 0, E * D), "bq": (32, 0, FH * STRIP), "bk": (64, 0, FH * STRIP),
        "bv": (96, 0, D), "bo": (96, D, D), "bg": (96, 2 * D, E)}
ONES = E * D
BIAS_N = ONES + P

C_ID, C_COL, C_IOTA = 0, P, P + 4
C_N = C_IOTA + E
C_MS, C_MT = C_N, C_N + P

SM_UNITS = [[(3, 0)], [(2, 0), (0, 3 * P)], [(1, 0)]]
ST_UNITS = [[(0, 0)], [(1, 0), (3, 3 * P)], [(2, 0)]]
ST_N = [S, S, 2 * P]
PT_AT = [0, S, 2 * S, S + 3 * P]


PERIOD, FIRST = 17.0, 6.5


def batch_steps():
    steps = {("ln",): -4.05, ("xT",): -3.6, ("keep",): -1.2, ("fv",): -0.75, ("cT",): 13.4, ("wo",): 13.6, ("x2T",): 15.0,
             ("gate",): 15.75, ("pick",): 16.1, ("norm",): 20.9}
    steps.update({("ln2",): steps["ln",] + 0.15, ("wo2",): steps["wo",] + 0.15, ("x2",): steps["wo",] + 0.16,
                  ("norm2",): steps["norm",] + 0.15, ("out",): steps["norm",] + 0.16})
    for h in range(H):
        steps.update({("tq", h): h + 0.35, ("tk", h): h + 0.15, ("mT", h): h + 2.4})
        for unit in range(3):
            steps["sm", h, unit] = h + 1.1 + 0.3 * unit
            steps["st", h, unit] = h + 3.2 + 0.28 * unit
    for c in range(PG):
        steps.update({("proj", c, 0): 2 * c - 1.85, ("proj", c, 1): 2 * c - 0.8, ("div", c): 2 * c + 6.85,
                      ("round", c): 2 * c + 6.9, ("attn", c): 2 * c + 7.7})
        for i in range(T):
            steps["inv", c, i] = 2 * c + 6.2 + 0.1 * i
            steps["pv", c, i] = 2 * c + 5.3 + 0.25 * i
    for t in range(T):
        steps.update({("v", t, 0): t + 0.95, ("v", t, 1): 7.0 + t, ("moe", t, 0): t + 16.3, ("moe", t, 1): t + 16.75})
    for g in range(G):
        at = F_RATE * g
        steps.update({("fq", g): at - 3.2, ("fk", g): at - 2.65, ("fmT", g): at + 0.4, ("fT", g): at + F_RATE + 2.25})
        for f in range(GH):
            for j in range(T):
                steps["fsm", g * GH + f, j] = at - F_RATE + 0.5 + (F_RATE - 0.4) / 16 * (f * T + j)
        for i in range(T):
            steps["fpv", g, i] = at + 1.0 + F_RATE / 4 * (i + 1.3)
            for f in range(GH):
                steps["fst", g, i, f] = at + 0.75 + F_RATE / 16 * (i * T + f)
    return steps


F_RATE = 2.4
TIME = batch_steps()
WK_KINDS = ("xT", "v", "fv", "fq", "fk", "proj", "tq", "tk", "sm", "fsm", "mT", "fmT", "fT", "attn", "cT", "wo", "x2T",
            "gate", "moe")
SPLIT_KINDS = ("xT", "fq", "fk", "tq", "tk", "cT", "x2T")


def ordered(time):
    plan, waiting = [], []
    for x in sorted(time, key=lambda x: time[x] + PERIOD * (time[x] < FIRST)):
        plan.append(x)
        if x[0] in WK_KINDS:
            plan += [("lo",) + y for y in waiting]
            waiting = [x] if x[0] in SPLIT_KINDS else []
    return plan + [("lo",) + y for y in waiting]


PLAN = ordered(TIME)
assert min(TIME.values()) >= FIRST - PERIOD and max(TIME.values()) < FIRST + PERIOD
EARLY = {x for x in PLAN if TIME[x[1:] if x[0] == "lo" else x] < FIRST}
PLAN_SET = set(PLAN)
POS = {x: n for n, x in enumerate(PLAN)}


def steps_of(*kinds):
    return [x for x in PLAN if x[0] in kinds]


WK_LIST = steps_of(*WK_KINDS)
ST_LIST = steps_of("st", "fst")
BANKS = 5
FILL = {"sm": 0.6, "fsm": 0.2, "fst": 0.25, "st": 0.8, "v": 0.65, "proj": 1.1, "fq": 0.8, "fk": 0.8, "moe": 0.8, "attn": 1.55,
        "pv": 1.0, "fpv": 0.15}
HOLD = {"sm": 1.2, "fsm": 1.2, "st": 1.0, "fst": 1.0, "moe": 2.2, "gate": 2.5, "wo": 4.0, "proj": 0.7}
HOLD.update({kind: 2.15 for kind in SPLIT_KINDS})


def banks():
    at, now, free = {}, 0.0, [0.0] * BANKS
    for x in PLAN:
        if x[0] in WK_KINDS + ("st", "fst"):
            i = free.index(min(free))
            now = max(now, free[i]) + FILL.get(x[0], 0.5)
            at[x], free[i] = i, now + HOLD.get(x[0], 1.2)
        else:
            now += FILL.get(x[0], 0.0)
    return at


BANK = banks()
USERS = [[x for x in PLAN if BANK.get(x) == i] for i in range(BANKS)]
PROJ_LIST = steps_of("proj")
Y_STEPS = steps_of("attn", "x2", "out")
NORMS = steps_of("ln", "ln2", "wo", "wo2", "norm", "norm2")
assert all(NORMS.index((x + "2",)) == NORMS.index((x,)) + 1 for x in ("ln", "wo", "norm"))
assert Y_STEPS[-1] == ("attn", PG - 1) and not EARLY & set(Y_STEPS)
CHAIN = {"ln": 2, "norm": 3, "inv": 1, "fT": 1, "wo": 2, "gate": 2, "pick": 9, "moe": 1}


class Turn:

    def __init__(self, b, steps):
        self.b, self.steps = b, steps

    def value(self, s, events, n_before, at):
        every = sum(events.values())
        if n_before == 0:
            return self.b * every + (2 * every + sum(n for x, n in events.items() if x in self.steps and POS[x] <= at))
        return self.b * every + (every + sum(n for x, n in events.items() if POS[x] <= at))


def build(nc, x, w_qkv, w_out, wq, bq, wk, bk, wv, bv, wo, bo, g1, be1, g2, be2, wg, bg, we, bexp, table, rope, out):
    with ExitStack() as ctx:
        def sb(name, shape, dt=F32):
            return ctx.enter_context(nc.sbuf_tensor(name, shape, dt))

        def sem(name):
            return ctx.enter_context(nc.semaphore(name))

        consts = sb("consts", [P, C_N])
        ident = consts[:, C_ID:C_ID + P]
        low_rows = consts[:, C_COL:C_COL + 1]
        q_low = consts[:, C_COL + 1:C_COL + 2]
        k_low = consts[:, C_COL + 2:C_COL + 3]
        second = consts[:, C_COL + 3:C_COL + 4]
        experts = consts[:, C_IOTA:C_IOTA + E]
        masks = sb("masks", [P, 3, P], BF16)
        angles = sb("angles", [P, T, 3 * DH // 2])
        wqkv_h = sb("wqkv_h", [P, 3 * H * DH], F32R)
        wqkv_l = sb("wqkv_l", [P, 3 * H * DH], F32R)
        wout_h = sb("wout_h", [P, PG, D], F32R)
        wout_l = sb("wout_l", [P, PG, D], F32R)
        we_h = sb("we_h", [P, E, D], F32R)
        we_l = sb("we_l", [P, E, D], F32R)
        small_h = sb("small_h", [P, 2 * D + E], F32R)
        small_l = sb("small_l", [P, 2 * D + E], F32R)
        strips_h = sb("strips_h", [P, 2, FH, STRIP], F32R)
        strips_l = sb("strips_l", [P, 2, FH, STRIP], F32R)
        affine = sb("affine", [P, 4, D])
        biases = sb("biases", [P, BIAS_N], F32R)

        x_in = sb("x_in", [P, T, D])
        xn = sb("xn", [P, T, D])
        xt_h = sb("xt_h", [P, S], F32R)
        xt_l = sb("xt_l", [P, S], F32R)
        v = sb("v", [P, T, H, DH])
        ones = sb("ones", [P, DH])
        fv = sb("fv", [P, T, FH, FVW])
        unrot = sb("unrot", [P, 2, 2 * PH * DH])
        rot = sb("rot", [P, 2, 2 * PH * DH])
        qk = sb("qk", [P, 2, T, 2 * PH, 2, DH])
        q_hl = sb("q_hl", [P, 4, S], F32R)
        q_hm = sb("q_hm", [P, 4, S], F32R)
        k_hh = sb("k_hh", [P, 4, S], F32R)
        k_l1 = sb("k_l1", [P, 4, S], F32R)
        fq = sb("fq", [P, 3, S], F32R)
        fk = sb("fk", [P, 3, S], F32R)
        nmax = sb("nmax", [P, 4, T])
        fnmax = sb("fnmax", [P, T, GH, STRIP])
        pt = sb("pt", [P, 3, 2 * S + 2 * P])
        fpt = sb("fpt", [P, 2, GH, S])
        fo = sb("fo", [P, S])
        frec = sb("frec", [P, T, GH])
        u = sb("u", [P, S])
        u_h = sb("u_h", [P, 2, S], F32R)
        u_l = sb("u_l", [P, 2, S], F32R)
        ct = sb("ct", [P, T, D])
        ct_h = sb("ct_h", [P, S], F32R)
        ct_l = sb("ct_l", [P, S], F32R)
        x2t_h, x2t_l = ct_h, ct_l
        part = sb("part", [P, T, D])
        y = sb("y", [P, T, D])
        branch = ct
        kept = sb("kept", [P, T, D])
        x2 = kept
        stats = sb("stats", [P, T, 6])
        moments = sb("moments", [P, T, 2])
        spread = sb("spread", [P, T])
        rstd = sb("rstd", [P, T])
        power = sb("power", [P, T])
        spare = sb("spare", [P, 1])
        early = part[:].rearrange("p t d -> p (t d)")[:, 0:7 * T * E].rearrange("p (a t e) -> p a t e", a=7, e=E)
        gmax = sb("gmax", [P, T])
        gsum = sb("gsum", [P, T])
        grec = sb("grec", [P, T])
        glog = early[:, 4]
        gexp = early[:, 5]
        gprob = early[:, 0]
        gtop = sb("gtop", [P, T, E])
        gidx = early[:, 6].bitcast(U32)
        gidf = early[:, 1]
        gate_a = early[:, 2]
        gate_b = early[:, 3]
        gate_w = sb("gate_w", [P, T, E])
        qk_flat = qk[:].rearrange("p a t h r d -> p (a t h r d)")
        rot_flat = rot[:].rearrange("p c n -> p (c n)")
        raw_qkv = fpt[:].rearrange("p a t n -> p (a t n)")[:, 0:3 * H * DH]
        raw_out = qk_flat[:, 0:PG * D].rearrange("p (c n) -> p c n", n=D)
        raw_we = qk_flat[:, PG * D:PG * D + E * D].rearrange("p (e n) -> p e n", n=D)
        raw_masks = qk_flat[:, (PG + E) * D:(PG + E + 2) * D].rearrange("p (c n) -> p c n", n=P)
        raw_small = rot_flat[:, 0:2 * D + E]
        raw_qk = unrot[:].rearrange("p k n -> p (k n)")[:, 0:2 * D]
        raw_bias = pt[:].rearrange("p a n -> p (a n)")[:, 0:BIAS_N]
        hi_bias = v[:].rearrange("p t h d -> p (t h d)")[:, 0:BIAS_N].bitcast(F32R)

        bank = [ctx.enter_context(nc.psum_tensor(f"bank{i}", [P, 512], F32)) for i in range(BANKS)]
        o_bank = ctx.enter_context(nc.psum_tensor("o_bank", [P, 512], F32))
        l_bank = ctx.enter_context(nc.psum_tensor("l_bank", [P, 512], F32))
        f_bank = ctx.enter_context(nc.psum_tensor("f_bank", [P, 512], F32))

        loaded = sem("loaded")
        w_loaded = sem("w_loaded")
        x_loaded = sem("x_loaded")
        out_sent = sem("out_sent")
        cleared = sem("cleared")
        prepared = sem("prepared")
        prep_pool = sem("prep_pool")
        prep_dve = sem("prep_dve")
        events = {}

        def per_turn(name, steps, n=1):
            s = sem(name)
            events[id(s)] = {x: n for x in steps}
            return s

        wk_full = per_turn("wk_full", WK_LIST)
        st_full = per_turn("st_full", ST_LIST)
        o_full = per_turn("o_full", [("pv", c, T - 1) for c in range(PG)])
        f_summed = per_turn("f_summed", steps_of("fpv"))
        rounded = per_turn("rounded", steps_of(*SPLIT_KINDS))
        v_copied = per_turn("v_copied", steps_of("v"))
        fv_copied = per_turn("fv_copied", [("fv",)])
        row_done = per_turn("row_done", steps_of("mT"))
        exp_done = per_turn("exp_done", ST_LIST)
        fo_done = per_turn("fo_done", [("fpv", g, T - 1) for g in range(G)])
        u_rounded = per_turn("u_rounded", steps_of("round"))
        gate_exp = per_turn("gate_exp", [("gate",)])
        split = per_turn("split", steps_of("lo"))
        copied = per_turn("copied", PROJ_LIST)
        product = per_turn("product", PROJ_LIST, 2)
        rotated = per_turn("rotated", PROJ_LIST, 2)
        variance = per_turn("variance", steps_of("ln", "wo", "norm"))
        rstd_done = per_turn("rstd_done", steps_of("ln", "wo", "norm"))
        max_done = per_turn("max_done", steps_of("sm", "fsm"))
        fmax_done = per_turn("fmax_done", steps_of("fmT"))
        divided = per_turn("divided", steps_of("div"))
        u_split = per_turn("u_split", steps_of("round"))
        fdivided = per_turn("fdivided", steps_of("fT"))
        misc_read = per_turn("misc_read", steps_of("attn", "wo2", "gate", "moe"))
        normal = per_turn("normal", [("ln2",)])
        xn_kept = per_turn("xn_kept", [("keep",)])
        x2_done = per_turn("x2_done", [("x2",)])
        normed = per_turn("normed", [("norm2",)])
        y_added = per_turn("y_added", steps_of("x2", "out"))
        pool_step = per_turn("pool_step", steps_of("x2", "out"), 2)
        logits = per_turn("logits", [("gate",)])
        step_done = per_turn("step_done", [])
        events[id(step_done)] = {x: CHAIN[x[0]] for x in steps_of(*CHAIN)}

        def now(turn, s, x, less=0):
            return turn.value(s, events[id(s)], 0, POS[x]) - less

        def past(turn, s, x, less=0):
            return turn.value(s, events[id(s)], 1, POS[x]) - less

        def last(turn, x_, s, x, less=0):
            return now(turn, s, x, less) if POS[x] < POS[x_] else past(turn, s, x, less)

        def own(turn, x_, s, x, less=0, older=0):
            turns = older + (x in EARLY) - (x_ in EARLY)
            assert x in events[id(s)]
            assert turns > 0 or turns == 0 and POS[x] <= POS[x_], (x_, x)
            return now(turn, s, x, less) if turns == 0 else past(turn, s, x, less)

        def start(eng, *sems):
            for s in sems:
                eng.sem_inc(s, sum(events[id(s)].values()))

        def fill_up(eng, *sems):
            eng.drain()
            for s in sems:
                left = sum(n for x, n in events[id(s)].items() if x not in EARLY)
                if left:
                    eng.sem_inc(s, left)

        def bank_of(x):
            return bank[BANK[x]]

        def bank_read(turn, x):
            users = USERS[BANK[x]]
            n = users.index(x) - 1
            while n >= 0 and users[n] not in turn.steps:
                n -= 1
            user = users[n]
            reader = {"proj": copied, "mT": row_done, "fmT": fmax_done, "fT": fdivided, "sm": max_done, "fsm": max_done,
                      "st": exp_done, "fst": exp_done, "fv": fv_copied, "v": v_copied}.get(user[0], misc_read)
            if user[0] in SPLIT_KINDS:
                reader, user = split, ("lo",) + user
            if user[0] == "wo":
                user = ("wo2",)
            return reader, now(turn, reader, user) if n >= 0 else past(turn, reader, user)

        x_tiles = x.rearrange("b (t p) d -> b p t d", p=P)
        out_tiles = out.rearrange("b (t p) d -> b p t d", p=P)
        N_LOADS = 4 + 1 + 4 + 6

        FIRST_PART = Turn(-1, EARLY)
        LAST = Turn(B - 1, set(PLAN) - EARLY)
        assert ("attn", 0) not in EARLY and ("ln",) in EARLY

        block = ctx.enter_context(nc.Block())

        @block.sync
        def _(sp):
            sp.dma_start(x_in[:], x_tiles[0]).then_inc(x_loaded, 16)
            for dst, src in ((consts[:], table[:, 0:C_N]),
                             (raw_masks, table[:, C_MS:C_MS + 2 * P].rearrange("p (c n) -> p c n", n=P)),
                             (raw_qk[:, 0:D], wq), (raw_qk[:, D:2 * D], wk)):
                sp.dma_start(dst, src).then_inc(loaded, 16)
            sp.wait_ge(cleared, 1)
            for name, a in (("bv", bv), ("bo", bo), ("bg", bg), ("bexp", bexp.rearrange("e d -> (e d)")), ("bq", bq), ("bk", bk)):
                p0, at, n = BIAS[name]
                if name in ("bq", "bk"):
                    at, n = S, D
                sp.dma_start(raw_bias[p0:p0 + 2, at:at + n], a.rearrange("(a d) -> a d", a=1).broadcast_to([2, n])).then_inc(loaded, 16)
            sp.dma_start(angles[:], rope.rearrange("(t p) c -> p t c", p=P)).then_inc(loaded, 16)
            for n, a in enumerate((g1, be1, g2, be2)):
                sp.dma_start(affine[:, n, :], a.rearrange("(a d) -> a d", a=1).broadcast_to([P, D])).then_inc(loaded, 16)
            with sp.Fori(0, B - 1) as b:
                sp.wait_ge(misc_read, now(Turn(b, PLAN_SET), misc_read, ("attn", 0)))
                sp.dma_start(x_in[:], x_tiles[bass.ds(b + 1, 1)].rearrange("b p t d -> p (b t) d")).then_inc(x_loaded, 16)
                sp.wait_ge(misc_read, now(Turn(b, PLAN_SET), misc_read, ("attn", PG - 1)))
                sp.dma_start(out_tiles[bass.ds(b, 1)].rearrange("b p t d -> p (b t) d"), y[:]).then_inc(out_sent, 16)
            sp.wait_ge(misc_read, now(LAST, misc_read, ("attn", PG - 1)))
            sp.dma_start(out_tiles[B - 1], y[:]).then_inc(out_sent, 16)
            sp.wait_ge(out_sent, 16 * (B + 1))

        @block.gpsimd
        def _(pool):
            nc.gpsimd.memset(power[:], -0.5).then_inc(prep_pool, 1)
            pool.wait_ge(prep_pool, 1)
            start(pool, pool_step, x2_done, y_added, product, rotated, rstd_done, u_split)

            def step(turn, x_):
                kind = x_[0]
                if kind == "proj":
                    _, g, pair = x_
                    pool.wait_ge(copied, now(turn, copied, x_))
                    if pair == 0:
                        old = ("tk", PH * ((g - 2) % PG) + PH - 1)
                        pool.wait_ge(wk_full, own(turn, x_, wk_full, old, older=int(g < 2)))
                    for k in range(2):
                        t = 2 * pair + k
                        cos = angles[:, t, 0:DH // 2].unsqueeze(1).unsqueeze(3).broadcast_to([P, 2 * PH, DH // 2, 2])
                        sin = angles[:, t, DH // 2:].unsqueeze(1).broadcast_to([P, 2 * PH, DH])
                        if k == 0:
                            pool.wait_ge(rotated, last(turn, x_, rotated, PROJ_LIST[PROJ_LIST.index(x_) - 1]))
                        else:
                            pool.wait_ge(rotated, now(turn, rotated, x_, 1))
                        nc.gpsimd.tensor_tensor(rot[:, 0].rearrange("p (h i two) -> p h i two", two=2, i=DH // 2),
                                                unrot[:, k].rearrange("p (h i two) -> p h i two", two=2, i=DH // 2), cos,
                                                ALU.mult)
                        nc.gpsimd.tensor_tensor(rot[:, 1].rearrange("p (h d) -> p h d", d=DH),
                                                unrot[:, k].rearrange("p (h d) -> p h d", d=DH), sin,
                                                ALU.mult).then_inc(product, 1)
                        pool.wait_ge(product, now(turn, product, x_, 1 - k))
                        shape = [P, 2 * PH, 2, DH // 2]
                        c, s_ = (rot[:, m].rearrange("p (h i two) -> p h i two", two=2, i=DH // 2) for m in range(2))
                        dst = qk[:, g % 2, t].rearrange("p h r (two i) -> p h r two i", two=2)
                        nc.gpsimd.tensor_tensor(
                            dst[:, :, :, 0], c[:, :, :, 0].unsqueeze(2).broadcast_to(shape),
                            s_[:, :, :, 1].unsqueeze(2).broadcast_to(shape), ALU.add)
                        nc.gpsimd.tensor_tensor(
                            dst[:, :, :, 1], c[:, :, :, 1].unsqueeze(2).broadcast_to(shape),
                            s_[:, :, :, 0].unsqueeze(2).broadcast_to(shape), ALU.add).then_inc(rotated, 1)
                elif kind == "round":
                    c = x_[1]
                    pool.wait_ge(u_rounded, now(turn, u_rounded, x_))
                    nc.gpsimd.tensor_tensor(u_l[:, c % 2], u[:], u_h[:, c % 2].bitcast(F32), ALU.subtract)\
                        .then_inc(u_split, 1)
                elif kind in ("ln", "wo", "norm"):
                    pool.wait_ge(variance, now(turn, variance, x_))
                    nc.gpsimd.tensor_tensor(rstd[:], spread[:], power[:], ALU.pow).then_inc(rstd_done, 1)

                elif kind in ("x2", "out"):
                    if kind == "x2":
                        pool.wait_ge(misc_read, own(turn, x_, misc_read, ("wo2",)))
                        n = 0
                    else:
                        pool.wait_ge(normed, own(turn, x_, normed, ("norm2",)))
                        n = 2
                    nc.gpsimd.tensor_tensor(branch[:], branch[:], affine[:, n].unsqueeze(1).broadcast_to([P, T, D]),
                                            ALU.mult).then_inc(pool_step, 1)
                    pool.wait_ge(pool_step, now(turn, pool_step, x_, 1))
                    nc.gpsimd.tensor_tensor(branch[:], branch[:], affine[:, n + 1].unsqueeze(1).broadcast_to([P, T, D]),
                                            ALU.add).then_inc(pool_step, 1)
                    pool.wait_ge(pool_step, now(turn, pool_step, x_))
                    if kind == "x2":
                        pool.wait_ge(xn_kept, own(turn, x_, xn_kept, ("keep",)))
                        nc.gpsimd.tensor_tensor(x2[:], branch[:], kept[:], ALU.add).then_inc(x2_done, 1)
                        pool.wait_ge(x2_done, now(turn, x2_done, x_))
                    else:
                        pool.wait_ge(y_added, own(turn, x_, y_added, ("x2",)))
                    pool.wait_ge(misc_read, last(turn, x_, misc_read, [z for z in Y_STEPS if z[0] == "attn" and POS[z] < POS[x_]][-1]))
                    nc.gpsimd.tensor_tensor(y[:], (x2 if kind == "x2" else branch)[:], y[:], ALU.add).then_inc(y_added, 1)

            for x_ in PLAN:
                if x_ in EARLY:
                    step(FIRST_PART, x_)
            fill_up(pool, pool_step, x2_done, y_added, product, rotated, rstd_done, u_split)
            with pool.Fori(0, B - 1) as b:
                for x_ in PLAN:
                    step(Turn(b, PLAN_SET), x_)
            for x_ in PLAN:
                if x_ not in EARLY:
                    step(LAST, x_)

        @block.scalar
        def _(act):
            for dst, src in ((raw_qkv, w_qkv), (raw_out, w_out.rearrange("(c p) n -> p c n", p=P)),
                             (raw_we, we.rearrange("e d f -> d e f")), (raw_small[:, 0:D], wv),
                             (raw_small[:, D:2 * D], wo), (raw_small[:, 2 * D:2 * D + E], wg)):
                act.dma_start(dst, src).then_inc(w_loaded, 16)
            act.wait_ge(w_loaded, 16 * 6)
            nc.scalar.copy(wqkv_h[:], raw_qkv).then_inc(prepared, 1)
            nc.scalar.copy(wout_h[:], raw_out).then_inc(prepared, 1)
            nc.scalar.copy(we_h[:], raw_we).then_inc(prepared, 1)
            nc.scalar.copy(small_h[:], raw_small).then_inc(prepared, 1)
            start(act, rounded, copied, v_copied, fv_copied, row_done, exp_done, fo_done, u_rounded, xn_kept, gate_exp)

            def step(turn, x_):
                kind = x_[0]
                if kind in SPLIT_KINDS:
                    act.wait_ge(wk_full, now(turn, wk_full, x_))
                    if kind == "xT":
                        user = max(("fk", G - 1), ("proj", PG - 1, 1), ("v", T - 1, 1), key=TIME.get)
                        act.wait_ge(wk_full, own(turn, x_, wk_full, user, older=1))
                        dst = xt_h[:]
                    elif kind in ("fq", "fk"):
                        g = x_[1]
                        user = g - 3 if g >= 3 else G - 1 if g == 0 else g
                        act.wait_ge(st_full, own(turn, x_, st_full, ("fst", user, T - 1, GH - 1), older=int(g < 3)))
                        dst = (fq if kind == "fq" else fk)[:, g % 3]
                    elif kind in ("tq", "tk"):
                        h = x_[1]
                        act.wait_ge(st_full, own(turn, x_, st_full, ("st", (h - 4) % H, 2), older=int(h < 4)))
                        dst = (q_hm if kind == "tq" else k_hh)[:, h % 4]
                    elif kind == "cT":
                        act.wait_ge(wk_full, own(turn, x_, wk_full, ("moe", T - 1, 1), older=1))
                        dst = ct_h[:]
                    else:
                        act.wait_ge(wk_full, own(turn, x_, wk_full, ("wo",)))
                        dst = x2t_h[:]
                    nc.scalar.copy(dst, bank_of(x_)[:]).then_inc(rounded, 1)
                elif kind == "v":
                    _, t, half = x_
                    act.wait_ge(wk_full, now(turn, wk_full, x_))
                    if t == 0:
                        act.wait_ge(o_full, own(turn, x_, o_full, ("pv", (1 + half) * PG // 2 - 1, T - 1), older=1))
                    nc.scalar.copy(v[:, t, half * H // 2:(half + 1) * H // 2],
                                   bank_of(x_)[:].rearrange("p (h d) -> p h d", d=DH)).then_inc(v_copied, 1)
                elif kind == "fv":
                    act.wait_ge(wk_full, now(turn, wk_full, x_))
                    act.wait_ge(f_summed, own(turn, x_, f_summed, ("fpv", G - 1, T - 1), older=1))
                    nc.scalar.copy(fv[:, :, :, 0:FD], bank_of(x_)[:].rearrange("p (t h d) -> p t h d", t=T, d=FD))\
                        .then_inc(fv_copied, 1)
                elif kind == "mT":
                    act.wait_ge(wk_full, now(turn, wk_full, x_))
                    nc.scalar.copy(q_hm[64:65, x_[1] % 4], bank_of(x_)[64:65, :]).then_inc(row_done, 1)
                elif kind == "st":
                    _, h, unit = x_
                    act.wait_ge(st_full, now(turn, st_full, x_))
                    if unit == 0:
                        user = h - 3 if h >= 3 else max(n for n in range(H) if n % 3 == h)
                        act.wait_ge(o_full, own(turn, x_, o_full, ("pv", user // 2, T - 1), older=int(h < 3)))
                    nc.scalar.activation(pt[:, h % 3, PT_AT[unit]:PT_AT[unit] + ST_N[unit]],
                                         bank_of(x_)[:, 0:ST_N[unit]],
                                         ACT.Exp, scale=1.0 / math.sqrt(DH)).then_inc(exp_done, 1)
                elif kind == "fst":
                    _, g, i, f = x_
                    act.wait_ge(st_full, now(turn, st_full, x_))
                    if f == 0:
                        m = (g * T + i - 2) % (G * T)
                        act.wait_ge(f_summed, own(turn, x_, f_summed, ("fpv", m // T, m % T), older=int(g == 0 and i < 2)))
                    nc.scalar.activation(fpt[:, i % 2, f], bank_of(x_)[:],
                                         ACT.Exp, scale=1.0 / math.sqrt(FD)).then_inc(exp_done, 1)
                elif kind == "fpv" and x_[2] == T - 1:
                    g = x_[1]
                    act.wait_ge(f_summed, now(turn, f_summed, x_))
                    act.wait_ge(wk_full, own(turn, x_, wk_full, ("fT", (g - 1) % G), older=int(g == 0)))
                    nc.scalar.copy(fo[:], f_bank[:]).then_inc(fo_done, 1)
                elif kind == "proj":
                    act.wait_ge(wk_full, now(turn, wk_full, x_))
                    act.wait_ge(rotated, last(turn, x_, rotated, PROJ_LIST[PROJ_LIST.index(x_) - 1]))
                    nc.scalar.copy(unrot[:].rearrange("p k n -> p (k n)"), bank_of(x_)[:]).then_inc(copied, 1)
                elif kind == "round":
                    c = x_[1]
                    act.wait_ge(divided, own(turn, x_, divided, ("div", c)))
                    act.wait_ge(wk_full, own(turn, x_, wk_full, ("attn", (c - 2) % PG), older=int(c < 2)))
                    nc.scalar.copy(u_h[:, c % 2], u[:]).then_inc(u_rounded, 1)
                elif kind == "keep":
                    act.wait_ge(normal, own(turn, x_, normal, ("ln2",)))
                    act.wait_ge(wk_full, own(turn, x_, wk_full, ("x2T",), older=1))
                    act.wait_ge(y_added, own(turn, x_, y_added, ("x2",), older=1))
                    nc.scalar.copy(kept[:], xn[:]).then_inc(xn_kept, 1)
                elif kind == "gate":
                    act.wait_ge(logits, now(turn, logits, x_))
                    nc.scalar.activation(gexp, glog, ACT.Exp).then_inc(gate_exp, 1)

            for x_ in PLAN:
                if x_ in EARLY:
                    step(FIRST_PART, x_)
            fill_up(act, rounded, copied, v_copied, fv_copied, row_done, exp_done, fo_done, u_rounded, xn_kept, gate_exp)
            with act.Fori(0, B - 1) as b:
                for x_ in PLAN:
                    step(Turn(b, PLAN_SET), x_)
            for x_ in PLAN:
                if x_ not in EARLY:
                    step(LAST, x_)

        @block.vector
        def _(dve):
            nc.vector.memset(raw_bias, 0.0).then_inc(cleared, 1)
            nc.vector.memset(fnmax[:], 0.0)
            nc.vector.memset(k_l1[:].bitcast(F32), 1.0)
            nc.vector.memset(ones[:], 1.0)
            nc.vector.memset(f_bank[:], 0.0)
            nc.vector.memset(fv[:].rearrange("p t h d -> p (t h) d")[:, :, FD:FVW], 1.0)
            nc.vector.memset(strips_h[:].bitcast(F32), 0.0)
            nc.vector.memset(strips_l[:].bitcast(F32), 0.0).then_inc(prep_dve, 1)
            dve.wait_ge(loaded, 16 * N_LOADS)
            row_k, at_k, n_k = BIAS["bk"]
            nc.vector.memset(raw_bias[row_k:row_k + 1, at_k:at_k + n_k].rearrange("p (h c) -> p h c", c=STRIP)[:, :, 0:1],
                             1.0).then_inc(prep_dve, 1)
            for p0, at, _ in (BIAS["bq"], BIAS["bk"]):
                strip = raw_bias[p0:p0 + 2, at:at + FH * STRIP].rearrange("p (h c) -> p h c", c=STRIP)
                for c in range(1, 4):
                    nc.vector.tensor_copy(strip[:, :, c * FD:(c + 1) * FD],
                                          raw_bias[p0:p0 + 2, S:S + D].rearrange("p (h d) -> p h d", d=FD)).then_inc(prep_dve, 1)
            nc.vector.tensor_copy(masks[:, 0], ident)
            nc.vector.tensor_copy(masks[:, 1:3], raw_masks)
            dve.wait_ge(prep_dve, 8)
            nc.vector.tensor_copy(hi_bias, raw_bias).then_inc(prep_dve, 1)
            dve.wait_ge(prep_dve, 9)
            nc.vector.scalar_tensor_tensor(out=biases[:], in0=hi_bias.bitcast(F32), scalar=second, in1=raw_bias,
                                           op0=ALU.mult, op1=ALU.add).then_inc(prep_dve, 1)
            dve.wait_ge(prep_dve, 10)
            nc.vector.memset(biases[:, ONES:BIAS_N].bitcast(F32), 1.0)
            nc.vector.memset(biases[BIAS["bq"][0]:BIAS["bq"][0] + 2, S:2 * S].bitcast(F32), 1.0)
            nc.vector.memset(biases[BIAS["bk"][0]:BIAS["bk"][0] + 2, S:2 * S].bitcast(F32), 1.0)
            for n in range(2):
                src = raw_qk[:, n * D:(n + 1) * D].rearrange("p (h d) -> p h d", d=FD)
                for c in range(1, 4):
                    nc.vector.tensor_copy(strips_h[:, n, :, c * FD:(c + 1) * FD], src).then_inc(prep_dve, 1)
            dve.wait_ge(prep_dve, 16)
            for n in range(2):
                src = raw_qk[:, n * D:(n + 1) * D].rearrange("p (h d) -> p h d", d=FD)
                for c in range(1, 4):
                    nc.vector.tensor_tensor(strips_l[:, n, :, c * FD:(c + 1) * FD], src,
                                            strips_h[:, n, :, c * FD:(c + 1) * FD].bitcast(F32), ALU.subtract)
            dve.wait_ge(prepared, 4)
            nc.vector.tensor_tensor(wqkv_l[:], raw_qkv, wqkv_h[:].bitcast(F32), ALU.subtract)
            nc.vector.tensor_tensor(wout_l[:], raw_out, wout_h[:].bitcast(F32), ALU.subtract)
            nc.vector.tensor_tensor(we_l[:], raw_we, we_h[:].bitcast(F32), ALU.subtract)
            nc.vector.tensor_tensor(small_l[:], raw_small, small_h[:].bitcast(F32), ALU.subtract).then_inc(prep_dve, 1)
            dve.wait_ge(prep_dve, 17)
            dve.drain().then_inc(prepared, 1)
            start(dve, split, variance, max_done, fmax_done, divided, fdivided, misc_read, normal, normed, logits,
                  step_done)

            def carry_wait():
                nc.vector.memset(spare[:], 0.0)

            chain = [None, 0]

            def link(turn):
                chain[1] -= 1
                return now(turn, step_done, chain[0], chain[1])

            def layernorm(turn, x_, src):
                for t in range(T - 1):
                    nc.vector.bn_stats(stats[:, t], src(t))
                nc.vector.bn_stats(stats[:, T - 1], src(T - 1)).then_inc(step_done, 1)
                dve.wait_ge(step_done, link(turn))
                carry_wait()
                for t in range(T - 1):
                    nc.vector.bn_aggr(moments[:, t], stats[:, t])
                nc.vector.bn_aggr(moments[:, T - 1], stats[:, T - 1]).then_inc(step_done, 1)
                dve.wait_ge(step_done, link(turn))
                nc.vector.tensor_scalar(spread[:].unsqueeze(2), moments[:, :, 1:2], EPS, None, ALU.add).then_inc(variance, 1)

            def step(turn, x_):
                kind = x_[0]
                assert chain[1] == 0, x_
                chain[0], chain[1] = x_, events[id(step_done)].get(x_, 0)
                if kind in WK_KINDS and kind not in SPLIT_KINDS + ("proj", "mT", "v", "fv"):
                    dve.wait_ge(wk_full, now(turn, wk_full, x_))
                if kind == "ln":
                    dve.wait_ge(x_loaded, turn.b * 16 + 32)
                    layernorm(turn, x_, lambda t: x_in[:, t])
                elif kind == "ln2":
                    dve.wait_ge(rstd_done, own(turn, x_, rstd_done, ("ln",)))
                    dve.wait_ge(wk_full, own(turn, x_, wk_full, ("xT",), older=1))
                    dve.wait_ge(xn_kept, own(turn, x_, xn_kept, ("keep",), older=1))
                    for t in range(T - 1):
                        nc.vector.tensor_scalar(xn[:, t], x_in[:, t], moments[:, t, 0:1], rstd[:, t:t + 1],
                                                ALU.subtract, ALU.mult)
                    nc.vector.tensor_scalar(xn[:, T - 1], x_in[:, T - 1], moments[:, T - 1, 0:1], rstd[:, T - 1:T],
                                            ALU.subtract, ALU.mult).then_inc(normal, 1)
                elif kind == "lo":
                    kind, of = x_[1], x_[1:]
                    dve.wait_ge(rounded, own(turn, x_, rounded, of))
                    src = bank_of(of)[:]
                    if kind == "xT":
                        ins = nc.vector.tensor_tensor(xt_l[:], src, xt_h[:].bitcast(F32), ALU.subtract)
                    elif kind in ("fq", "fk"):
                        strips = (fq if kind == "fq" else fk)[:, of[1] % 3]
                        ins = nc.vector.scalar_tensor_tensor(
                            out=strips, in0=strips.bitcast(F32), scalar=q_low if kind == "fq" else k_low, in1=src,
                            op0=ALU.mult, op1=ALU.add)
                    elif kind == "tq":
                        h = of[1]
                        ins = nc.vector.scalar_tensor_tensor(out=q_hl[:, h % 4], in0=q_hm[:, h % 4].bitcast(F32),
                                                             scalar=low_rows, in1=src, op0=ALU.mult, op1=ALU.add)
                    elif kind == "tk":
                        h = of[1]
                        ins = nc.vector.tensor_tensor(k_l1[0:DH, h % 4], src[0:DH], k_hh[0:DH, h % 4].bitcast(F32),
                                                      ALU.subtract)
                    else:
                        ins = nc.vector.tensor_tensor(ct_l[:], src, ct_h[:].bitcast(F32), ALU.subtract)
                    ins.then_inc(split, 1)
                elif kind == "sm":
                    _, h, unit = x_
                    if unit == 0:
                        dve.wait_ge(wk_full, own(turn, x_, wk_full, ("mT", (h - 4) % H), older=int(h < 4)))
                    units = SM_UNITS[unit]
                    for j, at in units[:-1]:
                        nc.vector.tensor_reduce(nmax[:, h % 4, j:j + 1], bank_of(x_)[:, at:at + (j + 1) * P],
                                                AX.X, ALU.max, negate=True)
                    j, at = units[-1]
                    nc.vector.tensor_reduce(nmax[:, h % 4, j:j + 1], bank_of(x_)[:, at:at + (j + 1) * P],
                                            AX.X, ALU.max, negate=True).then_inc(max_done, 1)
                elif kind == "fsm":
                    _, f, j = x_
                    if f % GH == 0 and j == 0:
                        g = f // GH
                        dve.wait_ge(wk_full, own(turn, x_, wk_full, ("fmT", (g - 1) % G), older=int(g == 0)))
                    nc.vector.tensor_reduce(fnmax[:, j, f % GH, 0:1], bank_of(x_)[:], AX.X, ALU.max, negate=True)\
                        .then_inc(max_done, 1)
                elif kind == "fmT":
                    g = x_[1]
                    nc.vector.tensor_tensor(fq[:, g % 3], bank_of(x_)[:], fq[:, g % 3].bitcast(F32), ALU.add).then_inc(fmax_done, 1)
                elif kind == "inv":
                    _, c, i = x_
                    if i == 0:
                        dve.wait_ge(o_full, own(turn, x_, o_full, ("pv", c, T - 1)))
                        dve.wait_ge(u_split, own(turn, x_, u_split, ("round", (c - 1) % PG), older=int(c == 0)))
                    tok = slice(i * P, (i + 1) * P)
                    nc.vector.reciprocal(u[:, tok], l_bank[:, tok]).then_inc(step_done, 1)
                    link(turn)
                elif kind == "div":
                    c = x_[1]
                    dve.wait_ge(step_done, own(turn, x_, step_done, ("inv", c, T - 1)))
                    nc.vector.tensor_tensor(u[:], o_bank[:], u[:], ALU.mult).then_inc(divided, 1)
                elif kind == "fT":
                    g = x_[1]
                    bank = bank_of(x_)[:].rearrange("p (t f c) -> p t f c", f=GH, c=STRIP)
                    nc.vector.reciprocal(frec[:].unsqueeze(3), bank[:, :, :, FD:FVW]).then_inc(step_done, 1)
                    dve.wait_ge(step_done, link(turn))
                    if g == 0:
                        dve.wait_ge(y_added, own(turn, x_, y_added, ("out",), older=1))
                        dve.wait_ge(wk_full, own(turn, x_, wk_full, ("cT",), older=1))
                    nc.vector.tensor_tensor(
                        ct[:, :, g * GH * FD:(g + 1) * GH * FD].rearrange("p t (f d) -> p t f d", d=FD),
                        bank[:, :, :, 0:FD], frec[:].unsqueeze(3).broadcast_to([P, T, GH, FD]), ALU.mult).then_inc(fdivided, 1)
                elif kind == "attn":
                    src = bank_of(x_)[:].rearrange("p (t d) -> p t d", d=D)
                    if x_[1] == 0:
                        dve.wait_ge(out_sent, turn.b * 16 + 16)
                        nc.vector.tensor_tensor(y[:], src, x_in[:], ALU.add).then_inc(misc_read, 1)
                    else:
                        before = Y_STEPS[Y_STEPS.index(x_) - 1]
                        done = misc_read if before[0] == "attn" else y_added
                        dve.wait_ge(done, own(turn, x_, done, before))
                        nc.vector.tensor_tensor(y[:], src, y[:], ALU.add).then_inc(misc_read, 1)
                elif kind == "wo":
                    src = bank_of(x_)[:].rearrange("p (t d) -> p t d", d=D)
                    layernorm(turn, x_, lambda t: src[:, t])
                elif kind == "wo2":
                    src = bank_of(("wo",))[:].rearrange("p (t d) -> p t d", d=D)
                    dve.wait_ge(rstd_done, own(turn, x_, rstd_done, ("wo",)))
                    for t in range(T - 1):
                        nc.vector.tensor_scalar(branch[:, t], src[:, t], moments[:, t, 0:1], rstd[:, t:t + 1],
                                                ALU.subtract, ALU.mult)
                    nc.vector.tensor_scalar(branch[:, T - 1], src[:, T - 1], moments[:, T - 1, 0:1], rstd[:, T - 1:T],
                                            ALU.subtract, ALU.mult).then_inc(misc_read, 1)
                elif kind == "gate":
                    src = bank_of(x_)[:, 0:T * E].rearrange("p (t e) -> p t e", e=E)
                    wide = [P, T, E]
                    nc.vector.tensor_reduce(gmax[:].unsqueeze(2), src, AX.X, ALU.max, negate=True).then_inc(step_done, 1)
                    dve.wait_ge(step_done, link(turn))
                    nc.vector.tensor_tensor(glog, src, gmax[:].unsqueeze(2).broadcast_to(wide), ALU.add).then_inc(step_done, 1)
                    dve.wait_ge(step_done, link(turn))
                    nc.vector.memset(gtop[:], 0.0).then_inc(misc_read, 1)
                    nc.vector.memset(gidx, 0).then_inc(logits, 1)
                elif kind == "pick":
                    wide = [P, T, E]
                    dve.wait_ge(gate_exp, own(turn, x_, gate_exp, ("gate",)))
                    nc.vector.tensor_reduce(gsum[:].unsqueeze(2), gexp, AX.X, ALU.add).then_inc(step_done, 1)
                    dve.wait_ge(step_done, link(turn))
                    nc.vector.reciprocal(grec[:], gsum[:]).then_inc(step_done, 1)
                    dve.wait_ge(step_done, link(turn))
                    nc.vector.tensor_tensor(gprob, gexp, grec[:].unsqueeze(2).broadcast_to(wide), ALU.mult)\
                        .then_inc(step_done, 1)
                    dve.wait_ge(step_done, link(turn))
                    carry_wait()
                    for t in range(T - 1):
                        nc.vector.max(gtop[:, t], gprob[:, t])
                    nc.vector.max(gtop[:, T - 1], gprob[:, T - 1]).then_inc(step_done, 1)
                    dve.wait_ge(step_done, link(turn))
                    carry_wait()
                    for t in range(T - 1):
                        nc.vector.max_index(gidx[:, t], gtop[:, t], gprob[:, t])
                    nc.vector.max_index(gidx[:, T - 1], gtop[:, T - 1], gprob[:, T - 1]).then_inc(step_done, 1)
                    dve.wait_ge(step_done, link(turn))
                    nc.vector.tensor_copy(gidf, gidx).then_inc(step_done, 1)
                    dve.wait_ge(step_done, link(turn))
                    iota = experts.unsqueeze(1).broadcast_to(wide)
                    nc.vector.tensor_tensor(gate_a, iota, gidf[:, :, 0:1].broadcast_to(wide), ALU.is_equal)
                    nc.vector.tensor_tensor(gate_b, iota, gidf[:, :, 1:2].broadcast_to(wide), ALU.is_equal)\
                        .then_inc(step_done, 1)
                    dve.wait_ge(step_done, link(turn))
                    nc.vector.tensor_tensor(gate_a, gate_a, gtop[:, :, 0:1].broadcast_to(wide), ALU.mult)
                    nc.vector.tensor_tensor(gate_b, gate_b, gtop[:, :, 1:2].broadcast_to(wide), ALU.mult)\
                        .then_inc(step_done, 1)
                    dve.wait_ge(step_done, link(turn))
                    nc.vector.tensor_tensor(gate_w[:], gate_a, gate_b, ALU.add).then_inc(step_done, 1)
                    dve.wait_ge(step_done, link(turn))
                elif kind == "moe":
                    if x_[1:] == (0, 0):
                        dve.wait_ge(x2_done, own(turn, x_, x2_done, ("x2",)))
                    _, t, half = x_
                    w = gate_w[:, t, half * HALF:(half + 1) * HALF].unsqueeze(2).broadcast_to([P, HALF, D])
                    products = bank_of(x_)[:].rearrange("p (e d) -> p e d", d=D)
                    nc.vector.tensor_tensor(products, products, w, ALU.mult).then_inc(step_done, 1)
                    dve.wait_ge(step_done, link(turn))
                    into = (branch, part)[half]
                    nc.vector.tensor_reduce(into[:, t].unsqueeze(2), products.rearrange("p e d -> p d e"),
                                            AX.X, ALU.add).then_inc(misc_read, 1)
                elif kind == "norm":
                    dve.wait_ge(misc_read, own(turn, x_, misc_read, ("moe", T - 1, 1)))
                    nc.vector.tensor_tensor(branch[:], branch[:], part[:], ALU.add).then_inc(step_done, 1)
                    dve.wait_ge(step_done, link(turn))
                    layernorm(turn, x_, lambda t: branch[:, t])
                elif kind == "norm2":
                    dve.wait_ge(rstd_done, own(turn, x_, rstd_done, ("norm",)))
                    for t in range(T - 1):
                        nc.vector.tensor_scalar(branch[:, t], branch[:, t], moments[:, t, 0:1], rstd[:, t:t + 1],
                                                ALU.subtract, ALU.mult)
                    nc.vector.tensor_scalar(branch[:, T - 1], branch[:, T - 1], moments[:, T - 1, 0:1], rstd[:, T - 1:T],
                                            ALU.subtract, ALU.mult).then_inc(normed, 1)

            for x_ in PLAN:
                if x_ in EARLY:
                    step(FIRST_PART, x_)
            fill_up(dve, split, variance, max_done, fmax_done, divided, fdivided, misc_read, normal, normed, logits,
                  step_done)
            with dve.Fori(0, B - 1) as b:
                for x_ in PLAN:
                    step(Turn(b, PLAN_SET), x_)
            for x_ in PLAN:
                if x_ not in EARLY:
                    step(LAST, x_)

        @block.tensor
        def _(pe):
            start(pe, wk_full, st_full, o_full, f_summed)
            pe.sem_inc(out_sent, 16)
            pe.wait_ge(prepared, 5)

            def split3(dst, lh, ll, rh, rl, bias=None):
                nc.tensor.matmul(dst, lh, rh, start=True, stop=False)
                nc.tensor.matmul(dst, ll, rh, start=False, stop=False)
                ins = nc.tensor.matmul(dst, lh, rl, start=False, stop=bias is None)
                if bias is not None:
                    ins = nc.tensor.matmul(dst, bias[0], bias[1], start=False, stop=True)
                return ins

            def bias_rows(name, a=0, n=None):
                p0, at, whole = BIAS[name]
                return biases[p0:p0 + 2, at + a:at + a + (n or whole)]

            def one_rows(name):
                return biases[BIAS[name][0]:BIAS[name][0] + 2, ONES:ONES + P]

            def transposed(bank, src):
                for t in range(T):
                    n = src(t).shape[-1]
                    ins = nc.tensor.transpose(bank[0:n, t * P:(t + 1) * P], src(t), ident)
                return ins

            def step(turn, x_):
                kind = x_[0]
                if x_ in BANK:
                    read, value = bank_read(turn, x_)
                    pe.wait_ge(read, value)
                    psum = bank_of(x_)
                if kind in ("fq", "fk", "proj", "v", "fv"):
                    pe.wait_ge(split, own(turn, x_, split, ("lo", "xT")))
                if kind == "xT":
                    pe.wait_ge(normal, own(turn, x_, normal, ("ln2",)))
                    transposed(psum, lambda t: xn[:, t]).then_inc(wk_full, 1)
                elif kind == "v":
                    _, t, half = x_
                    a = 2 * H * DH + half * 512
                    tok = slice(t * P, (t + 1) * P)
                    split3(psum[:], xt_h[:, tok], xt_l[:, tok], wqkv_h[:, a:a + 512], wqkv_l[:, a:a + 512]).then_inc(wk_full, 1)
                elif kind == "fv":
                    for t in range(T):
                        tok = slice(t * P, (t + 1) * P)
                        ins = split3(psum[:, tok], xt_h[:, tok], xt_l[:, tok], small_h[:, 0:D], small_l[:, 0:D],
                                     (one_rows("bv"), bias_rows("bv")))
                    ins.then_inc(wk_full, 1)
                elif kind in ("fq", "fk"):
                    g, n = x_[1], int(kind == "fk")
                    wh = strips_h[:, n, g * GH:(g + 1) * GH].rearrange("p h c -> p (h c)")
                    wl = strips_l[:, n, g * GH:(g + 1) * GH].rearrange("p h c -> p (h c)")
                    name = "bk" if n else "bq"
                    split3(psum[:], wh, wl, xt_h[:], xt_l[:], (bias_rows(name, g * P, P),
                           biases[BIAS[name][0]:BIAS[name][0] + 2, S:2 * S])).then_inc(wk_full, 1)
                elif kind == "proj":
                    _, g, pair = x_
                    n = PH * DH
                    w = [a[:].rearrange("p (k n) -> p k n", n=H * DH)[:, 0:2, g * n:(g + 1) * n] for a in (wqkv_h, wqkv_l)]
                    for t in range(2 * pair, 2 * pair + 2):
                        tok, at = slice(t * P, (t + 1) * P), t % 2 * 2 * n
                        ins = split3(psum[:, at:at + 2 * n], xt_h[:, tok], xt_l[:, tok], w[0], w[1])
                    ins.then_inc(wk_full, 1)
                elif kind in ("tq", "tk"):
                    h = x_[1]
                    g, k = h // PH, int(kind == "tk")
                    if h % PH == 0:
                        pe.wait_ge(rotated, own(turn, x_, rotated, ("proj", g, 1)))
                    transposed(psum, lambda t: qk[:, g % 2, t, k * PH + h % PH].rearrange("p r d -> p (r d)")).then_inc(wk_full, 1)
                elif kind == "mT":
                    h = x_[1]
                    pe.wait_ge(max_done, own(turn, x_, max_done, ("sm", h, 2)))
                    transposed(psum, lambda t: nmax[:, h % 4, t:t + 1].broadcast_to([P, DH + 1])).then_inc(wk_full, 1)
                elif kind == "fmT":
                    g = x_[1]
                    pe.wait_ge(max_done, own(turn, x_, max_done, ("fsm", GH * g + GH - 1, T - 1)))
                    transposed(psum, lambda t: fnmax[:, t].rearrange("p h c -> p (h c)")).then_inc(wk_full, 1)
                elif kind == "sm":
                    _, h, unit = x_
                    if unit == 0:
                        pe.wait_ge(split, own(turn, x_, split, ("lo", "tk", h)))
                    for j, at in SM_UNITS[unit]:
                        nc.tensor.matmul(psum[:, at:at + (j + 1) * P], q_hl[:, h % 4, j * P:(j + 1) * P],
                                         k_hh[:, h % 4, 0:(j + 1) * P], start=True, stop=True)
                        ins = nc.tensor.matmul(psum[:, at + j * P:at + (j + 1) * P], masks[:, 0], masks[:, 1],
                                               start=False, stop=True, skip_group_check=True)
                    ins.then_inc(wk_full, 1)
                elif kind == "fsm":
                    _, f, j = x_
                    g, r = f // GH, slice(f % GH * STRIP, (f % GH + 1) * STRIP)
                    if f % GH == 0 and j == 0:
                        pe.wait_ge(split, own(turn, x_, split, ("lo", "fk", g)))
                    nc.tensor.matmul(psum[:], fq[r, g % 3, j * P:(j + 1) * P], fk[r, g % 3], start=True, stop=True,
                                     tile_position=(r.start, 0)).then_inc(wk_full, 1)
                elif kind == "st":
                    _, h, unit = x_
                    if unit == 0:
                        pe.wait_ge(row_done, own(turn, x_, row_done, ("mT", h)))
                    for i, at in ST_UNITS[unit]:
                        dst = psum[:, at:at + S - i * P]
                        nc.tensor.matmul(dst, k_hh[:, h % 4, i * P:(i + 1) * P], q_hl[:, h % 4, i * P:S],
                                         start=True, stop=False)
                        nc.tensor.matmul(dst, k_l1[0:DH + 1, h % 4, i * P:(i + 1) * P], q_hm[0:DH + 1, h % 4, i * P:S],
                                         start=False, stop=True)
                        ins = nc.tensor.matmul(dst[:, 0:P], masks[:, 0], masks[:, 2],
                                               start=False, stop=True, skip_group_check=True)
                    ins.then_inc(st_full, 1)
                elif kind == "fst":
                    _, g, i, f = x_
                    r = slice(f * STRIP, (f + 1) * STRIP)
                    if i == 0 and f == 0:
                        pe.wait_ge(fmax_done, own(turn, x_, fmax_done, ("fmT", g)))
                    nc.tensor.matmul(psum[:], fk[r, g % 3, i * P:(i + 1) * P], fq[r, g % 3],
                                     start=True, stop=True, tile_position=(r.start, 0)).then_inc(st_full, 1)
                elif kind == "pv":
                    _, c, i = x_
                    if i == 0:
                        pe.wait_ge(exp_done, own(turn, x_, exp_done, ("st", 2 * c + 1, 2)))
                        pe.wait_ge(divided, own(turn, x_, divided, ("div", (c - 1) % PG), older=int(c == 0)))
                        if c in (0, PG // 2):
                            pe.wait_ge(v_copied, own(turn, x_, v_copied, ("v", T - 1, c // (PG // 2))))
                    for bank, sums in ((o_bank, False), (l_bank, True)):
                        for r in range(2):
                            h = 2 * c + r
                            ins = nc.tensor.matmul(bank[r * DH:(r + 1) * DH, i * P:S], ones[:] if sums else v[:, i, h],
                                                   pt[:, h % 3, PT_AT[i]:PT_AT[i] + S - i * P],
                                                   start=(i == 0), stop=(i == T - 1), tile_position=(0, r * DH))
                    if i == T - 1:
                        ins.then_inc(o_full, 1)
                elif kind == "fpv":
                    _, g, i = x_
                    pe.wait_ge(exp_done, own(turn, x_, exp_done, ("fst", g, i, GH - 1)))
                    if i == 0:
                        pe.wait_ge(fo_done, own(turn, x_, fo_done, ("fpv", (g - 1) % G, T - 1), older=int(g == 0)))
                        if g == 0:
                            pe.wait_ge(fv_copied, own(turn, x_, fv_copied, ("fv",)))
                    for f in range(GH):
                        ins = nc.tensor.matmul(f_bank[f * STRIP:f * STRIP + FVW], fv[:, i, g * GH + f], fpt[:, i % 2, f],
                                               start=(i == 0), stop=(i == T - 1), tile_position=(0, f * STRIP))
                    ins.then_inc(f_summed, 1)
                elif kind == "fT":
                    g = x_[1]
                    pe.wait_ge(fo_done, own(turn, x_, fo_done, ("fpv", g, T - 1)))
                    transposed(psum, lambda t: fo[:, t * P:(t + 1) * P]).then_inc(wk_full, 1)
                elif kind == "attn":
                    c = x_[1]
                    pe.wait_ge(u_rounded, own(turn, x_, u_rounded, ("round", c)))
                    pe.wait_ge(u_split, own(turn, x_, u_split, ("round", c)))
                    for t in range(T):
                        tok = slice(t * P, (t + 1) * P)
                        ins = split3(psum[:, tok], u_h[:, c % 2, tok], u_l[:, c % 2, tok], wout_h[:, c], wout_l[:, c])
                    ins.then_inc(wk_full, 1)
                elif kind == "cT":
                    pe.wait_ge(fdivided, own(turn, x_, fdivided, ("fT", G - 1)))
                    transposed(psum, lambda t: ct[:, t]).then_inc(wk_full, 1)
                elif kind == "wo":
                    pe.wait_ge(split, own(turn, x_, split, ("lo", "cT")))
                    for t in range(T):
                        tok = slice(t * P, (t + 1) * P)
                        ins = split3(psum[:, tok], ct_h[:, tok], ct_l[:, tok], small_h[:, D:2 * D], small_l[:, D:2 * D],
                                     (one_rows("bo"), bias_rows("bo")))
                    ins.then_inc(wk_full, 1)
                elif kind == "x2T":
                    pe.wait_ge(x2_done, own(turn, x_, x2_done, ("x2",)))
                    transposed(psum, lambda t: x2[:, t]).then_inc(wk_full, 1)
                elif kind == "gate":
                    pe.wait_ge(split, own(turn, x_, split, ("lo", "x2T")))
                    for t in range(T):
                        tok = slice(t * P, (t + 1) * P)
                        ins = split3(psum[:, t * E:(t + 1) * E], x2t_h[:, tok], x2t_l[:, tok],
                                     small_h[:, 2 * D:2 * D + E], small_l[:, 2 * D:2 * D + E],
                                     (one_rows("bg"), bias_rows("bg")))
                    ins.then_inc(wk_full, 1)
                elif kind == "moe":
                    _, t, half = x_
                    tok = slice(t * P, (t + 1) * P)
                    e = slice(half * HALF, (half + 1) * HALF)
                    split3(psum[:], x2t_h[:, tok], x2t_l[:, tok], we_h[:, e].rearrange("p e d -> p (e d)"),
                           we_l[:, e].rearrange("p e d -> p (e d)"),
                           (one_rows("bexp"), bias_rows("bexp", half * 512, 512))).then_inc(wk_full, 1)

            for x_ in PLAN:
                if x_ in EARLY:
                    step(FIRST_PART, x_)
            fill_up(pe, wk_full, st_full, o_full, f_summed)
            with pe.Fori(0, B - 1) as b:
                for x_ in PLAN:
                    step(Turn(b, PLAN_SET), x_)
            for x_ in PLAN:
                if x_ not in EARLY:
                    step(LAST, x_)


_INS = ["L0_attn_x", "L0_attn_W_qkv", "L0_attn_W_out", "L0_ffn_Wq", "L0_ffn_bq", "L0_ffn_Wk", "L0_ffn_bk", "L0_ffn_Wv",
        "L0_ffn_bv", "L0_ffn_Wo", "L0_ffn_bo", "L0_ffn_g1", "L0_ffn_be1", "L0_ffn_g2", "L0_ffn_be2", "L0_ffn_Wg",
        "L0_ffn_bg", "L0_ffn_We", "L0_ffn_bexp"]


def _tables():
    import numpy as np

    table = np.zeros((P, C_MT + P), np.float32)
    p, n = np.arange(P)[:, None], np.arange(P)[None, :]
    table[:, C_ID:C_ID + P] = p == n
    table[:, C_MS:C_MS + P] = np.where(n > p, -1e30, 0)
    table[:, C_MT:C_MT + P] = np.where(p > n, -1e30, 0)
    row = np.arange(P) % STRIP
    table[:, C_COL] = np.where(np.arange(P) >= DH, -1, 0)
    table[:, C_COL + 1] = np.where((row >= 2 * FD) & (row < 3 * FD), -1, 0)
    table[:, C_COL + 2] = np.where(row >= 3 * FD, -1, 0)
    table[:, C_COL + 3] = np.where(row == 1, -1, 0)
    table[:, C_IOTA:C_IOTA + E] = np.arange(E)
    pairs = np.arange(0, DH, 2).astype(np.float32)
    freqs = (np.float32(1.0) / np.float32(10000.0) ** (pairs / np.float32(DH))).astype(np.float32)
    angle = (np.arange(S).astype(np.float32)[:, None] * freqs[None, :]).astype(np.float32)
    sines = np.stack([np.sin(angle), -np.sin(angle)], 2).reshape(S, DH)
    rope = np.concatenate([np.cos(angle), sines], 1).astype(np.float32)
    return table, rope


def kernel(**inputs):
    import numpy as _np
    import concourse.bacc as _bacc
    from concourse import mybir as _mybir
    from concourse.bass_utils import run_bass_kernel_spmd as _run

    nc = _bacc.Bacc("TRN2", target_bir_lowering=False, num_devices=1)
    table, rope = _tables()
    given = {name: _np.ascontiguousarray(inputs[name]) for name in _INS}
    given["table"], given["rope"] = table, rope
    arrays, args = {}, []
    for name, a in given.items():
        arrays[f"in_{name}_dram"] = a
        args.append(nc.dram_tensor(f"in_{name}_dram", a.shape, _mybir.dt.from_np(a.dtype), kind="ExternalInput").ap())
    args.append(nc.dram_tensor("out_0_dram", (B, S, D), _mybir.dt.float32, kind="ExternalOutput").ap())
    build(nc, *args)
    r = _run(nc, [arrays], core_ids=[0])
    return r.results[0]["out_0_dram"]
```
